# Optimizing a Trainium2 kernel written in Bass

```python
import numpy as np
import jax
import jax.numpy as jnp

def _softmax(x, axis=-1):
    return jax.nn.softmax(x, axis=axis)

def _gelu(x):
    return jax.nn.gelu(x, approximate=True)

def _silu(x):
    return jax.nn.silu(x)

def _sigmoid(x):
    return jax.nn.sigmoid(x)

def _layernorm(x, axis=-1, eps=1e-05):
    m = jnp.mean(x, axis=axis, keepdims=True)
    v = jnp.var(x, axis=axis, keepdims=True)
    return (x - m) / jnp.sqrt(v + eps)

def _scatter_add(tgt, idx, src, axis=0):
    return tgt.at[idx].add(src)

def _segment_sum(src, seg, n):
    return jax.ops.segment_sum(src, seg, n)
kernel_name = 'mk_vit_tower_d1_tok_img256_r4_cb7ea9'

def setup_inputs(seed: int=0):
    np.random.seed(seed)
    _w = jnp.asarray

    def _rec_inputs():
        import jax
        import jax.numpy as jnp
        _rk = jax.random.key(seed)
        x = -7.10856e-05 + 0.999911 * jax.random.normal(jax.random.fold_in(_rk, 1), (4, 64, 128, 64), jnp.float32)
        return x
    x = _rec_inputs()

    def _L0_tok_setup():
        import jax, jax.numpy as jnp
        import numpy as np
        PATCH_LEN = 16
        STRIDE = 8
        PAD = 8
        key = jax.random.key(seed)
        k1, k2 = jax.random.split(key)
        x = jax.random.normal(k1, (32, 64, 128, 64), dtype=jnp.float32)
        in_feat = 64 * (PATCH_LEN // 2 + 1) * 2
        W = jax.random.normal(k2, (64, in_feat), dtype=jnp.float32) * 0.02
        return {'x': x, 'W': W}
    _L0_tok_all = _L0_tok_setup()
    _L0_tok_in = {k: v for k, v in _L0_tok_all.items() if k in ('W',)}
    del _L0_tok_all

    def _L0_attn_setup():
        import jax, jax.numpy as jnp
        import numpy as np
        GROUPS = 64
        EPS = 1e-05
        DIM = 64
        SEQ = 256
        BATCH = 1

        def _group_norm(y, weight, bias):
            g = y.reshape(y.shape[:-1] + (GROUPS, -1))
            mean = g.mean(axis=-1, keepdims=True)
            var = g.var(axis=-1, keepdims=True)
            g = (g - mean) * jax.lax.rsqrt(var + EPS)
            return g.reshape(y.shape) * weight + bias

        def gate_loop_operator(k, v, q, a):
            kv = (k[..., :, None] * v[..., None, :]).astype(a.dtype)
            aa = a[..., :, None]

            def binop(e_i, e_j):
                a_i, kv_i = e_i
                a_j, kv_j = e_j
                return (a_j * a_i, a_j * kv_i + kv_j)
            _, y = jax.lax.associative_scan(binop, (aa, kv), axis=1)
            y = jnp.real(y).astype(k.dtype)
            return jnp.einsum('bld,blde->ble', q, y)
        key = jax.random.key(seed)
        ks = jax.random.split(key, 7)
        ortho = jax.nn.initializers.orthogonal()
        return {'x': jax.random.normal(ks[0], (BATCH, SEQ, DIM), jnp.float32), 'wq': ortho(ks[1], (DIM, DIM), jnp.float32), 'wk': ortho(ks[2], (DIM, DIM), jnp.float32), 'wv': ortho(ks[3], (DIM, DIM), jnp.float32), 'wa': ortho(ks[4], (DIM, 2 * DIM), jnp.float32), 'wg': ortho(ks[5], (DIM, DIM), jnp.float32), 'wo': ortho(ks[6], (DIM, DIM), jnp.float32), 'gn_weight': jnp.ones((DIM,), jnp.float32), 'gn_bias': jnp.zeros((DIM,), jnp.float32), 'bias': jnp.zeros((DIM,), jnp.float32)}
    _L0_attn_all = _L0_attn_setup()
    _L0_attn_in = {k: v for k, v in _L0_attn_all.items() if k in ('wq', 'wk', 'wv', 'wa', 'wg', 'wo', 'gn_weight', 'gn_bias', 'bias')}
    del _L0_attn_all

    def _L0_ffn_setup():
        import jax, jax.numpy as jnp
        import numpy as np
        B, T, D, H, E = (16, 1024, 64, 128, 8)
        key = jax.random.key(seed)
        ks = jax.random.split(key, 5)
        x = jax.random.normal(ks[0], (B, T, D), dtype=jnp.float32)
        gate_w = jax.random.normal(ks[1], (D, E), dtype=jnp.float32) * 0.02
        gate_b = jnp.zeros((E,), dtype=jnp.float32)
        W1 = jax.random.normal(ks[2], (E, D, H), dtype=jnp.float32) * 0.02
        b1 = jnp.zeros((E, H), dtype=jnp.float32)
        W2 = jax.random.normal(ks[3], (E, H, D), dtype=jnp.float32) * 0.02
        b2 = jnp.zeros((E, D), dtype=jnp.float32)
        return {'x': x, 'gate_w': gate_w, 'gate_b': gate_b, 'W1': W1, 'b1': b1, 'W2': W2, 'b2': b2}
    _L0_ffn_all = _L0_ffn_setup()
    _L0_ffn_in = {k: v for k, v in _L0_ffn_all.items() if k in ('gate_w', 'gate_b', 'W1', 'b1', 'W2', 'b2')}
    del _L0_ffn_all
    return {'x': x, 'L0_tok_W': _L0_tok_in['W'], 'L0_attn_wq': _L0_attn_in['wq'], 'L0_attn_wk': _L0_attn_in['wk'], 'L0_attn_wv': _L0_attn_in['wv'], 'L0_attn_wa': _L0_attn_in['wa'], 'L0_attn_wg': _L0_attn_in['wg'], 'L0_attn_wo': _L0_attn_in['wo'], 'L0_attn_gn_weight': _L0_attn_in['gn_weight'], 'L0_attn_gn_bias': _L0_attn_in['gn_bias'], 'L0_attn_bias': _L0_attn_in['bias'], 'L0_ffn_gate_w': _L0_ffn_in['gate_w'], 'L0_ffn_gate_b': _L0_ffn_in['gate_b'], 'L0_ffn_W1': _L0_ffn_in['W1'], 'L0_ffn_b1': _L0_ffn_in['b1'], 'L0_ffn_W2': _L0_ffn_in['W2'], 'L0_ffn_b2': _L0_ffn_in['b2']}

def reference(x, L0_tok_W, L0_attn_wq, L0_attn_wk, L0_attn_wv, L0_attn_wa, L0_attn_wg, L0_attn_wo, L0_attn_gn_weight, L0_attn_gn_bias, L0_attn_bias, L0_ffn_gate_w, L0_ffn_gate_b, L0_ffn_W1, L0_ffn_b1, L0_ffn_W2, L0_ffn_b2):
    import jax
    import jax.numpy as jnp

    def _L0_tok_ref(x, W):
        import jax, jax.numpy as jnp
        import numpy as np
        PATCH_LEN = 16
        STRIDE = 8
        PAD = 8
        B, C, T, V = x.shape
        xp = jnp.pad(x, ((0, 0), (0, 0), (0, PAD), (0, 0)), mode='edge')
        Tp = T + PAD
        N = (Tp - PATCH_LEN) // STRIDE + 1
        idx = jnp.arange(N)[:, None] * STRIDE + jnp.arange(PATCH_LEN)[None, :]
        patches = xp[:, :, idx, :]
        patches = jnp.transpose(patches, (0, 4, 2, 3, 1))
        xf = jnp.fft.rfft(patches, axis=-2, norm='ortho')
        F = xf.shape[-2]
        x_real = xf.real.reshape(B, V, N, F * C)
        x_imag = xf.imag.reshape(B, V, N, F * C)
        x_emb = jnp.concatenate([x_real, x_imag], axis=-1)
        x_emb = x_emb @ W.T
        return x_emb.reshape(B, V * N, -1)

    def _L0_attn_ref(x, wq, wk, wv, wa, wg, wo, gn_weight, gn_bias, bias):
        import jax, jax.numpy as jnp
        import numpy as np
        GROUPS = 64
        EPS = 1e-05
        DIM = 64
        SEQ = 256
        BATCH = 1

        def _group_norm(y, weight, bias):
            g = y.reshape(y.shape[:-1] + (GROUPS, -1))
            mean = g.mean(axis=-1, keepdims=True)
            var = g.var(axis=-1, keepdims=True)
            g = (g - mean) * jax.lax.rsqrt(var + EPS)
            return g.reshape(y.shape) * weight + bias

        def gate_loop_operator(k, v, q, a):
            kv = (k[..., :, None] * v[..., None, :]).astype(a.dtype)
            aa = a[..., :, None]

            def binop(e_i, e_j):
                a_i, kv_i = e_i
                a_j, kv_j = e_j
                return (a_j * a_i, a_j * kv_i + kv_j)
            _, y = jax.lax.associative_scan(binop, (aa, kv), axis=1)
            y = jnp.real(y).astype(k.dtype)
            return jnp.einsum('bld,blde->ble', q, y)
        q = x @ wq
        k = x @ wk
        v = x @ wv
        g = x @ wg
        a = (x @ wa).astype(jnp.float32)
        a_real, a_imag = jnp.split(a, 2, axis=-1)
        a_complex = jax.nn.sigmoid(a_real) * jnp.exp(1j * a_imag)
        y = gate_loop_operator(k, v, q, a_complex)
        y = _group_norm(y, gn_weight, gn_bias)
        y = y * jax.nn.silu(g)
        return y @ wo + bias

    def _L0_ffn_ref(x, gate_w, gate_b, W1, b1, W2, b2):
        import jax, jax.numpy as jnp
        import numpy as np
        B, T, D, H, E = (16, 1024, 64, 128, 8)
        Bb, Tt, Dd = x.shape
        Ee = gate_w.shape[1]
        xf = x.reshape(-1, Dd)
        N = xf.shape[0]
        logits = xf @ gate_w + gate_b
        probs = jax.nn.softmax(logits, axis=-1)
        top2_vals, top2_idx = jax.lax.top_k(probs, 2)
        cw = jnp.zeros((N, Ee), dtype=xf.dtype).at[jnp.arange(N)[:, None], top2_idx].add(top2_vals)

        def step(acc, params):
            w1, bb1, w2, bb2, we = params
            h = jax.nn.gelu(xf @ w1 + bb1, approximate=False)
            y = h @ w2 + bb2
            return (acc + we[:, None] * y, None)
        out, _ = jax.lax.scan(step, jnp.zeros_like(xf), (W1, b1, W2, b2, cw.T))
        return out.reshape(Bb, Tt, Dd)
    h = _L0_tok_ref(x, L0_tok_W)
    h = h + _L0_attn_ref(_layernorm(h, axis=-1), L0_attn_wq, L0_attn_wk, L0_attn_wv, L0_attn_wa, L0_attn_wg, L0_attn_wo, L0_attn_gn_weight, L0_attn_gn_bias, L0_attn_bias)
    h = h + _L0_ffn_ref(_layernorm(h, axis=-1), L0_ffn_gate_w, L0_ffn_gate_b, L0_ffn_W1, L0_ffn_b1, L0_ffn_W2, L0_ffn_b2)
    return h

_drawn_inputs = setup_inputs


def setup_inputs(seed=0):
    import zlib

    import numpy as np

    out = dict(_drawn_inputs(seed))
    spreads = {'L0_attn_gn_weight': (1.0, 0.2),
     'L0_attn_gn_bias': (0.0, 0.1),
     'L0_attn_bias': (0.0, 0.1),
     'L0_ffn_gate_b': (0.0, 0.1),
     'L0_ffn_b1': (0.0, 0.8),
     'L0_ffn_b2': (0.0, 0.1)}
    factors = {'L0_ffn_W1': 6.915, 'L0_ffn_W2': 5.901}
    for name, (base, spread) in spreads.items():
        noise = np.random.default_rng([zlib.crc32(name.encode()), seed]).standard_normal(out[name].shape)
        drawn = base * np.exp(spread * noise) if base else spread * noise
        out[name] = jnp.asarray(drawn.astype(out[name].dtype))
    for name, factor in factors.items():
        out[name] = (out[name] * factor).astype(out[name].dtype)
    return out
```

```python
from contextlib import ExitStack

import concourse.bass as bass
from concourse import mybir

ALU = mybir.AluOpType
ACT = mybir.ActivationFunctionType
F32 = mybir.dt.float32
F32R = mybir.dt.float32r
BF16 = mybir.dt.bfloat16
AX_X = mybir.AxisListType.X

B, C, T, V = 4, 64, 128, 64
WIN, HOP = 16, 8
NF = WIN // 2 + 1
G = 2 * NF
NWIN = T // HOP
D = 64
E, H = 8, 128
EPS = 1e-5
P = 128
DLO = 4
DHI = D // DLO
NG = 8
NCH = 2 * B
CH = 512
NSPLIT = 3


def vit_layer(nc, x, W, wg, wo, gn_bias, attn_bias, gate_w, gate_b, W1, b1, W2, b2, dft, ident, center, rank, sel, out):
    ctx = ExitStack()
    with ctx:
        def sb(name, shape, dt=F32):
            return ctx.enter_context(nc.sbuf_tensor(name, shape, dt))

        def sem(name):
            return ctx.enter_context(nc.semaphore(name))

        x_sb = [[sb(f"x_{pair}_{par}", [P, NWIN + 1, 2, V]) for par in range(2)] for pair in range(2)]
        w_rows = sb("w_rows", [DLO * G, DHI, 2, C])
        dft_sb = sb("dft_sb", [DLO * G, DLO * WIN])
        w_eff = sb("w_eff", [P, 2, 4, D])
        hg_rhs = sb("hg_rhs", [P, 2 * P])
        center_sb = sb("center_sb", [P, P])
        wg_bd = sb("wg_bd", [P, P])
        wo_bd = sb("wo_bd", [P, P])
        gnb = sb("gnb", [P, 1])
        bias_b = sb("bias_b", [P, D])
        gate_b_b = sb("gate_b_b", [P, E])
        rank_b = sb("rank_b", [P, E])
        gw_raw = sb("gw_raw", [P, E])
        gw_r = sb("gw_r", [P, 2 * E], F32R)
        w1_raw = sb("w1_raw", [P, E, H])
        w1_hi = sb("w1_hi", [P, E, H], F32R)
        w1_lo = sb("w1_lo", [P, E, H], F32R)
        w2_sb = sb("w2_sb", [P, E, D])
        b1_sb = sb("b1_sb", [P, E])
        b2_raw = sb("b2_raw", [NSPLIT * E, D])
        b2_res = sb("b2_res", [NSPLIT * E, D])
        b2_sp = sb("b2_sp", [P, 4, D], BF16)
        sel_f = sb("sel_f", [NSPLIT * E, E, P])
        sel_sb = sb("sel_sb", [P, E, P], BF16)
        ident_bf = sb("ident_bf", [P, P], BF16)
        expo = sb("expo", [P, NG])

        hT_sb = sb("hT_sb", [P, CH])
        h_sb = sb("h_sb", [P, NG, D])
        hb_sb = sb("hb_sb", [P, NG, D])
        g_sb = sb("g_sb", [P, NG * D])
        th_sb = sb("th_sb", [P, NG * D])
        s_sb = sb("s_sb", [P, NG * D])
        sT_sb = sb("sT_sb", [P, CH])
        st1 = sb("st1", [P, NG, 6])
        st2 = sb("st2", [P, NG, 6])
        sm1 = sb("sm1", [P, 6, NG])
        sm2 = sb("sm2", [P, 6, NG])
        h2_all = sb("h2_all", [P, NCH * 4, D])
        xc_sb = sb("xc_sb", [P, NG, D])
        xn_sb = sb("xn_sb", [P, NG, D])
        split_sb = sb("split_sb", [P, NG, 2, D])
        xT_all = sb("xT_all", [P, NCH * CH], F32R)
        lz = sb("lz", [P, 8, NG, E])
        lm = sb("lm", [P, 8, NG])
        cw = sb("cw", [P, NG, E])
        cres = sb("cres", [P, NG, E])
        cw_sp = sb("cw_sp", [P, NG, NSPLIT, E], BF16)
        cwT_all = sb("cwT_all", [P, NCH * CH], BF16)
        act_sb = sb("act_sb", [P, 4, CH])
        acc_sb = sb("acc_sb", [P, CH])
        y_sb = sb("y_sb", [P, 4, D])
        o_sb = sb("o_sb", [P, 4, D])

        banks = [ctx.enter_context(nc.psum_tensor(f"bank{i}", [P, n * 512], F32)) for i, n in enumerate([2, 2, 1, 1, 1, 1])]
        HG_PS, XT_PS, ST_PS, WO_PS, HT_PS, LG_PS = banks
        A_PS = [HG_PS[:, 0:512], HG_PS[:, 512:1024], XT_PS[:, 0:512], XT_PS[:, 512:1024]]
        B_PS = [ST_PS[:, :], WO_PS[:, :]]
        CT_PS = XT_PS[0:NSPLIT * E, 0:512].bitcast(BF16)
        ACC_PS, OT_PS = HT_PS, LG_PS

        x_ld = [[sem(f"x_ld_{pair}_{par}") for par in range(2)] for pair in range(2)]
        w_ld, hgw_ld, wo_ld, vec_ld, gw_ld, w1_ld, w2_ld, b2_ld, sel_ld = (
            sem(n) for n in "w_ld hgw_ld wo_ld vec_ld gw_ld w1_ld w2_ld b2_ld sel_ld".split())
        zeroed = sem("zeroed")
        weff_mm, weff_ready = sem("weff_mm"), sem("weff_ready")
        wgc_mm, hg_rhs_ready = sem("wgc_mm"), sem("hg_rhs_ready")
        wo_ready, gw_ready, ident_bf_ready, w1_ready, sel_ready, b2_ready = (
            sem(n) for n in "wo_ready gw_ready ident_bf_ready w1_ready sel_ready b2_ready".split())
        xa_used, tok_done, hT_ready, hg_done, h_ready, var1, rstd1, g_ready, tanh_done = (
            sem(n) for n in "xa_used tok_done hT_ready hg_done h_ready var1 rstd1 g_ready tanh_done".split())
        s_ready, st_done, sT_ready, wo_done, hb_ready, h2_ready, var2, rstd2, xn_ready, xh_ready, xl_ready = (
            sem(n) for n in "s_ready st_done sT_ready wo_done hb_ready h2_ready var2 rstd2 xn_ready xh_ready xl_ready".split())
        xt_done, xT_ready, lg_done, z_ready, exp_done, cw_ready, ct_done, cwT_ready = (
            sem(n) for n in "xt_done xT_ready lg_done z_ready exp_done cw_ready ct_done cwT_ready".split())
        mm1_done, gelu_done, bc_done, scaled, mm2_done, acc_done, acc_ready, ot_done, y1_done, y_ready, out_st = (
            sem(n) for n in "mm1_done gelu_done bc_done scaled mm2_done acc_done acc_ready ot_done y1_done y_ready out_st".split())
        dve_step = sem("dve_step")

        def grp(ap):
            return ap.rearrange("p (j h d) -> p j h d", j=4, h=2)

        block = ctx.enter_context(nc.Block())

        @block.sync
        def _(sp):
            xv = x.rearrange("b c (m k s) v -> b c m k (s v)", k=4, s=2)
            for b in range(B):
                for pair in range(2):
                    if b >= 2:
                        sp.wait_ge(tok_done if pair else xa_used, b - 1)
                    dst = x_sb[pair][b % 2]
                    for half in range(2):
                        rows = slice(64 * half, 64 * half + 64)
                        sp.dma_start(dst[rows, 0:NWIN, :, :].rearrange("c m s v -> c m (s v)"),
                                     xv[b, :, :, 2 * half + pair, :]).then_inc(x_ld[pair][b % 2], 16)
                        sp.dma_start(dst[rows, NWIN, :, :], x[b, :, T - 1:T, :].to_broadcast([C, 2, V])
                                     ).then_inc(x_ld[pair][b % 2], 16)
            ov = out.rearrange("b (v h k j) d -> b h k v (j d)", h=2, k=2, j=4)
            with sp.Fori(0, B) as b:
                for hi in range(2):
                    sp.wait_ge(y_ready, 2 * b + hi + 1)
                    for j4 in range(2):
                        sp.dma_start(ov[b, hi, j4, :, :], o_sb[64 * j4:64 * j4 + 64, :, :].rearrange("v j d -> v (j d)")
                                     ).then_inc(out_st, 16)
            sp.wait_ge(out_st, 32 * NCH)

        @block.gpsimd
        def _(pool):
            for t in (wg_bd, wo_bd):
                nc.gpsimd.memset(t[:, :], 0.0).then_inc(zeroed, 1)
            nc.gpsimd.memset(b2_sp[:, :, :], 0.0).then_inc(zeroed, 1)
            nc.gpsimd.memset(expo[:, :], -0.5).then_inc(zeroed, 1)
            nc.gpsimd.memset(sel_sb[:, :, :], 0.0).then_inc(zeroed, 1)
            nc.gpsimd.memset(cwT_all[:, :], 0.0).then_inc(zeroed, 1)
            pool.wait_ge(zeroed, 6)
            pool.wait_ge(vec_ld, 16 * 6)

            def add_bias(b):
                pool.wait_ge(h_ready, b + 1)
                if b:
                    pool.wait_ge(h2_ready, b)
                nc.gpsimd.tensor_tensor(hb_sb[:, :, :], h_sb[:, :, :], bias_b[:, None, :].to_broadcast([P, NG, D]),
                                        ALU.add).then_inc(hb_ready, 1)

            def rsqrt(sm, ready, done, b):
                pool.wait_ge(ready, b + 1)
                nc.gpsimd.tensor_tensor(sm[:, 5, :], sm[:, 4, :], expo[:, :], ALU.pow).then_inc(done, 1)

            def low_part(b):
                pool.wait_ge(xn_ready, b + 1)
                pool.wait_ge(xh_ready, b + 1)
                nc.gpsimd.tensor_tensor(split_sb[:, :, 1, :], xn_sb[:, :, :], split_sb[:, :, 0, :], ALU.subtract
                                        ).then_inc(xl_ready, 1)

            for b in range(B + 1):
                if b < B:
                    rsqrt(sm1, var1, rstd1, b)
                if b >= 1:
                    rsqrt(sm2, var2, rstd2, b - 1)
                if b < B:
                    add_bias(b)
                if b >= 1:
                    low_part(b - 1)

        @block.scalar
        def _(act):
            wv = W.rearrange("(l h) (g c) -> l g h c", l=DLO, c=C)
            for l in range(DLO):
                for rep in range(2):
                    act.dma_start(w_rows[G * l:G * l + G, :, rep, :], wv[l]).then_inc(w_ld, 16)
            act.dma_start(dft_sb[:, :], dft).then_inc(w_ld, 16)
            act.dma_start(hg_rhs[:, 0:P], ident).then_inc(hgw_ld, 16)
            act.dma_start(center_sb[:, :], center).then_inc(hgw_ld, 16)
            act.wait_ge(zeroed, 4)
            for hi in range(2):
                act.dma_start(wg_bd[64 * hi:64 * hi + 64, 64 * hi:64 * hi + 64], wg).then_inc(hgw_ld, 16)
            for hi in range(2):
                act.dma_start(wo_bd[64 * hi:64 * hi + 64, 64 * hi:64 * hi + 64], wo).then_inc(wo_ld, 16)
                act.dma_start(gnb[64 * hi:64 * hi + 64, :], gn_bias.rearrange("(d o) -> d o", o=1)).then_inc(wo_ld, 16)
            act.dma_start(bias_b[:, :], attn_bias.rearrange("(o d) -> o d", o=1).to_broadcast([P, D])).then_inc(vec_ld, 16)
            act.dma_start(gate_b_b[:, :], gate_b.rearrange("(o e) -> o e", o=1).to_broadcast([P, E])).then_inc(vec_ld, 16)
            act.dma_start(rank_b[:, :], rank.to_broadcast([P, E])).then_inc(vec_ld, 16)
            act.dma_start(b1_sb[:, :], b1.rearrange("e h -> h e"), allow_slow_non_contiguous=True).then_inc(vec_ld, 16)
            for hi in range(2):
                act.dma_start(gw_raw[64 * hi:64 * hi + 64, :], gate_w).then_inc(vec_ld, 16)
                act.dma_start(w1_raw[64 * hi:64 * hi + 64, :, :], W1.rearrange("e d h -> d e h")).then_inc(w1_ld, 16)
            act.dma_start(w2_sb[:, :, :], W2.rearrange("e h d -> h e d")).then_inc(w2_ld, 16)
            act.dma_start(sel_f[:, :, :], sel).then_inc(sel_ld, 16)
            for i in range(NSPLIT):
                act.dma_start(b2_raw[E * i:E * i + E, :], b2).then_inc(b2_ld, 16)

            def evac_hT(b):
                act.wait_ge(tok_done, b + 1)
                if b:
                    act.wait_ge(hg_done, b)
                nc.scalar.activation(hT_sb[:, :], HT_PS[:, :], ACT.Copy).then_inc(hT_ready, 1)

            def evac_h(b):
                act.wait_ge(hg_done, b + 1)
                if b:
                    act.wait_ge(var1, b)
                    act.wait_ge(hb_ready, b)
                nc.scalar.activation(grp(h_sb[:, :, :].rearrange("p g d -> p (g d)")),
                                     HG_PS[:, :].rearrange("p (j k h d) -> p j k h d", j=4, k=2, h=2)[:, :, 0, :, :],
                                     ACT.Copy).then_inc(h_ready, 1)

            def tanh(b):
                act.wait_ge(g_ready, b + 1)
                if b:
                    act.wait_ge(s_ready, b)
                nc.scalar.activation(th_sb[:, :], g_sb[:, :], ACT.Tanh, scale=0.5).then_inc(tanh_done, 1)

            def evac_sT(b):
                act.wait_ge(st_done, b + 1)
                if b:
                    act.wait_ge(wo_done, b)
                nc.scalar.activation(sT_sb[:, :], ST_PS[:, :], ACT.Copy).then_inc(sT_ready, 1)

            def high_part(b):
                act.wait_ge(xn_ready, b + 1)
                if b:
                    act.wait_ge(xt_done, b)
                nc.scalar.activation(split_sb[:, :, 0, :].bitcast(F32R), xn_sb[:, :, :], ACT.Copy).then_inc(xh_ready, 1)

            def evac_xT(b):
                act.wait_ge(xt_done, b + 1)
                for k in range(2):
                    nc.scalar.activation(xT_all[:, (2 * b + k) * CH:(2 * b + k + 1) * CH],
                                         XT_PS[:, k * CH:(k + 1) * CH], ACT.Copy).then_inc(xT_ready, 1)

            def exp(b):
                act.wait_ge(z_ready, b + 1)
                nc.scalar.activation(lz[:, 2, :, :], lz[:, 1, :, :], ACT.Exp).then_inc(exp_done, 1)

            def evac_cwT(b):
                act.wait_ge(ct_done, b + 1)
                if b == 0:
                    act.wait_ge(zeroed, 6)
                nc.scalar.activation(cwT_all[0:NSPLIT * E, b * 2 * CH:(b + 1) * 2 * CH], CT_PS, ACT.Copy).then_inc(cwT_ready, 1)

            evac_hT(0)
            for b in range(B + 2):
                if b < B:
                    evac_h(b)
                if b >= 3:
                    evac_cwT(b - 3)
                if b < B:
                    tanh(b)
                if 1 <= b <= B:
                    high_part(b - 1)
                if b + 1 < B:
                    evac_hT(b + 1)
                if b < B:
                    evac_sT(b)
                if b >= 2:
                    exp(b - 2)
                if 1 <= b <= B:
                    evac_xT(b - 1)
            evac_cwT(B - 1)

            def moe(c):
                for e in range(E):
                    n = E * c + e
                    act.wait_ge(mm1_done, n + 1)
                    if e >= 4 or not isinstance(c, int) or c > 0:
                        act.wait_ge(mm2_done, n - 3)
                    nc.scalar.activation(act_sb[:, e % 4, :], A_PS[e % 4], ACT.Gelu, bias=b1_sb[:, e:e + 1]
                                         ).then_inc(gelu_done, 1)
                    if e == 1 and not (isinstance(c, int) and c == 0):
                        evac_acc(c - 1)

            def evac_acc(c):
                act.wait_ge(acc_done, c + 1)
                nc.scalar.activation(acc_sb[:, :], ACC_PS[:, :], ACT.Copy).then_inc(acc_ready, 1)

            moe(0)
            with act.Fori(1, NCH) as c:
                moe(c)
            evac_acc(NCH - 1)

        @block.vector
        def _(dve):
            steps = [0]

            def link(ins):
                steps[0] += 1
                ins.then_inc(dve_step, 1)
                dve.wait_ge(dve_step, steps[0])

            dve.wait_ge(weff_mm, 1)
            for half in range(2):
                rows = slice(64 * half, 64 * half + 64)
                for hop in range(2):
                    p0 = HOP * hop + 4 * half
                    src = HG_PS[rows, :].rearrange("c (h l p) -> c p l h", l=DLO, p=WIN)[:, p0:p0 + 4, :, :]
                    for s in range(4):
                        nc.vector.tensor_copy(w_eff[rows, hop, s, :].rearrange("c (l h) -> c l h", l=DLO), src[:, s, :, :]
                                              ).then_inc(weff_ready, 1)
            dve.wait_ge(wgc_mm, 1)
            nc.vector.tensor_copy(hg_rhs[:, P:2 * P], ST_PS[:, 0:P]).then_inc(hg_rhs_ready, 1)
            dve.wait_ge(wo_ld, 16 * 4)
            link(nc.vector.tensor_scalar(wo_bd[:, :], wo_bd[:, :], gnb[:, 0:1], 0.5, ALU.mult, ALU.mult))
            nc.vector.tensor_copy(ident_bf[:, :], hg_rhs[:, 0:P]).then_inc(wo_ready, 1)

            def prep_gate():
                dve.wait_ge(vec_ld, 16 * 6)
                link(nc.vector.tensor_copy(gw_r[:, 0:E], gw_raw[:, :]))
                nc.vector.tensor_tensor(gw_r[:, E:2 * E], gw_raw[:, :], gw_r[:, 0:E].bitcast(F32), ALU.subtract
                                        ).then_inc(gw_ready, 1)

            def prep_w1(part):
                es = slice(2 * part, 2 * part + 2)
                dve.wait_ge(w1_ld, 32)
                link(nc.vector.tensor_copy(w1_hi[:, es, :], w1_raw[:, es, :]))
                nc.vector.tensor_tensor(w1_lo[:, es, :], w1_raw[:, es, :], w1_hi[:, es, :].bitcast(F32), ALU.subtract
                                        ).then_inc(w1_ready, 1)

            def prep_sel_b2():
                dve.wait_ge(sel_ld, 16)
                dve.wait_ge(zeroed, 6)
                nc.vector.tensor_copy(sel_sb[0:NSPLIT * E, :, :], sel_f[:, :, :]).then_inc(sel_ready, 1)
                dve.wait_ge(b2_ld, 16 * NSPLIT)
                link(nc.vector.tensor_copy(b2_sp[0:NSPLIT * E, 0, :], b2_raw[:, :]))
                link(nc.vector.tensor_tensor(b2_res[:, :], b2_raw[:, :], b2_sp[0:NSPLIT * E, 0, :], ALU.subtract))
                link(nc.vector.tensor_copy(b2_sp[0:NSPLIT * E, 1, :], b2_res[:, :]))
                link(nc.vector.tensor_tensor(b2_raw[:, :], b2_res[:, :], b2_sp[0:NSPLIT * E, 1, :], ALU.subtract))
                nc.vector.tensor_copy(b2_sp[0:NSPLIT * E, 2, :], b2_raw[:, :]).then_inc(b2_ready, 1)

            def variance(src, st, sm, done, mean):
                for g in range(NG):
                    nc.vector.bn_stats(st[:, g, :], src[:, g, :]).then_inc(dve_step, 1)
                steps[0] += NG
                dve.wait_ge(dve_step, steps[0])
                me, m2e, mo, m2o = (st[:, :, k] for k in (1, 2, 4, 5))
                nc.vector.tensor_tensor(sm[:, 1, :], m2e, m2o, ALU.add).then_inc(dve_step, 1)
                if mean:
                    nc.vector.tensor_tensor(sm[:, 2, :], me, mo, ALU.add).then_inc(dve_step, 1)
                nc.vector.tensor_tensor(sm[:, 0, :], me, mo, ALU.subtract).then_inc(dve_step, 1)
                steps[0] += 3 if mean else 2
                dve.wait_ge(dve_step, steps[0])
                link(nc.vector.tensor_tensor(sm[:, 3, :], sm[:, 0, :], sm[:, 0, :], ALU.mult))
                link(nc.vector.scalar_tensor_tensor(sm[:, 0, :], sm[:, 3, :], D / 4.0, sm[:, 1, :], ALU.mult, ALU.add))
                if mean:
                    nc.vector.tensor_scalar(sm[:, 3, :], sm[:, 2, :], 0.5, None, ALU.mult).then_inc(dve_step, 1)
                    steps[0] += 1
                nc.vector.tensor_scalar(sm[:, 4, :], sm[:, 0, :], 1.0 / D, EPS, ALU.mult, ALU.add).then_inc(done, 1)

            def ln1_stats(b):
                dve.wait_ge(h_ready, b + 1)
                variance(h_sb, st1, sm1, var1, False)

            def scale_g(b):
                dve.wait_ge(rstd1, b + 1)
                dve.wait_ge(hg_done, b + 1)
                nc.vector.tensor_tensor(grp(g_sb[:, :]),
                                        HG_PS[:, :].rearrange("p (j k h d) -> p j k h d", j=4, k=2, h=2)[:, :, 1, :, :],
                                        sm1[:, 5, :].rearrange("p (j h o) -> p j h o", j=4, o=1).to_broadcast([P, 4, 2, D]),
                                        ALU.mult).then_inc(g_ready, 1)

            def silu(b):
                dve.wait_ge(tanh_done, b + 1)
                if b:
                    dve.wait_ge(st_done, b)
                nc.vector.scalar_tensor_tensor(s_sb[:, :], th_sb[:, :], 1.0, g_sb[:, :], ALU.add, ALU.mult
                                               ).then_inc(s_ready, 1)

            def residual(b):
                dve.wait_ge(wo_done, b + 1)
                dve.wait_ge(hb_ready, b + 1)
                nc.vector.tensor_tensor(h2_all[:, 8 * b:8 * b + 8, :].rearrange("p (h j) d -> p j h d", h=2),
                                        grp(WO_PS[:, :]), grp(hb_sb[:, :, :].rearrange("p g d -> p (g d)")),
                                        ALU.add).then_inc(h2_ready, 1)

            def ln2_stats(b):
                dve.wait_ge(h2_ready, b + 1)
                variance(h2_all[:, 8 * b:8 * b + 8, :], st2, sm2, var2, True)

            def ln2_center(b):
                dve.wait_ge(dve_step, steps[0])
                link(nc.vector.tensor_tensor(xc_sb[:, :, :], h2_all[:, 8 * b:8 * b + 8, :],
                                             sm2[:, 3, :, None].to_broadcast([P, NG, D]), ALU.subtract))

            def ln2_scale(b):
                dve.wait_ge(rstd2, b + 1)
                if b:
                    dve.wait_ge(xh_ready, b)
                    dve.wait_ge(xl_ready, b)
                nc.vector.tensor_tensor(xn_sb[:, :, :], xc_sb[:, :, :], sm2[:, 5, :, None].to_broadcast([P, NG, D]),
                                        ALU.mult).then_inc(xn_ready, 1)

            def logits(b):
                dve.wait_ge(lg_done, b + 1)
                lg = LG_PS[:, 0:NG * 2 * E].rearrange("p (g k e) -> p g k e", g=NG, k=2)
                link(nc.vector.tensor_tensor(lz[:, 0, :, :], lg[:, :, 0, :], gate_b_b[:, None, :].to_broadcast([P, NG, E]), ALU.add))
                link(nc.vector.tensor_tensor(lz[:, 3, :, :], lg[:, :, 1, :], lz[:, 0, :, :], ALU.add))
                link(nc.vector.tensor_reduce(lm[:, 0, :], lz[:, 3, :, :], AX_X, ALU.max))
                nc.vector.tensor_tensor(lz[:, 1, :, :], lz[:, 3, :, :], lm[:, 0, :, None].to_broadcast([P, NG, E]),
                                        ALU.subtract).then_inc(z_ready, 1)

            def routing(b):
                bc = [P, NG, E]

                def tt(o, a, c, op):
                    link(nc.vector.tensor_tensor(o, a, c, op))

                def first_max(p, one_hot, t, m):
                    link(nc.vector.tensor_reduce(lm[:, m, :], p, AX_X, ALU.max))
                    tt(lz[:, t, :, :], p, lm[:, m, :, None].to_broadcast(bc), ALU.is_equal)
                    tt(lz[:, t, :, :], lz[:, t, :, :], rank_b[:, None, :].to_broadcast(bc), ALU.mult)
                    link(nc.vector.tensor_reduce(lm[:, m + 1, :], lz[:, t, :, :], AX_X, ALU.max))
                    tt(one_hot, lz[:, t, :, :], lm[:, m + 1, :, None].to_broadcast(bc), ALU.is_equal)

                dve.wait_ge(exp_done, b + 1)
                ex, prob, hot1, hot2, rest, tmp = (lz[:, k, :, :] for k in (2, 4, 5, 6, 7, 3))
                link(nc.vector.tensor_reduce(lm[:, 1, :], ex, AX_X, ALU.add))
                link(nc.vector.reciprocal(lm[:, 2, :], lm[:, 1, :]))
                tt(prob, ex, lm[:, 2, :, None].to_broadcast(bc), ALU.mult)
                first_max(prob, hot1, 3, 3)
                link(nc.vector.scalar_tensor_tensor(rest, hot1, -2.0, prob, ALU.mult, ALU.add))
                first_max(rest, hot2, 3, 5)
                tt(tmp, hot1, hot2, ALU.add)
                tt(cw[:, :, :], prob, tmp, ALU.mult)
                if b:
                    dve.wait_ge(ct_done, b)
                link(nc.vector.tensor_copy(cw_sp[:, :, 0, :], cw[:, :, :]))
                tt(cres[:, :, :], cw[:, :, :], cw_sp[:, :, 0, :], ALU.subtract)
                link(nc.vector.tensor_copy(cw_sp[:, :, 1, :], cres[:, :, :]))
                tt(cw[:, :, :], cres[:, :, :], cw_sp[:, :, 1, :], ALU.subtract)
                nc.vector.tensor_copy(cw_sp[:, :, 2, :], cw[:, :, :]).then_inc(cw_ready, 1)

            for b in range(B + 2):
                if b < B:
                    ln1_stats(b)
                if 1 <= b <= B:
                    residual(b - 1)
                    ln2_stats(b - 1)
                if b < B:
                    scale_g(b)
                if 1 <= b <= B:
                    ln2_center(b - 1)
                if b == 0:
                    prep_gate()
                if b < B:
                    silu(b)
                if 1 <= b <= B:
                    ln2_scale(b - 1)
                if b >= 2:
                    logits(b - 2)
                    routing(b - 2)
                if b < 4:
                    prep_w1(b)
                if b == 2:
                    prep_sel_b2()

            def finish(c):
                dve.wait_ge(ot_done, c + 1)
                ot = OT_PS[:, :].rearrange("p (j k d) -> p j k d", j=4, k=2)
                nc.vector.tensor_tensor(y_sb[:, :, :], ot[:, :, 0, :], h2_all[:, bass.ts(c, 4), :], ALU.add
                                        ).then_inc(y1_done, 1)
                dve.wait_ge(y1_done, c + 1)
                if not (isinstance(c, int) and c == 0):
                    dve.wait_ge(out_st, 32 * c)
                nc.vector.tensor_tensor(o_sb[:, :, :], ot[:, :, 1, :], y_sb[:, :, :], ALU.add).then_inc(y_ready, 1)

            def moe(c):
                for e in range(E):
                    n = E * c + e
                    dve.wait_ge(gelu_done, n + 1)
                    dve.wait_ge(bc_done, n + 1)
                    nc.vector.tensor_tensor(act_sb[:, e % 4, :], act_sb[:, e % 4, :], B_PS[e % 2], ALU.mult
                                            ).then_inc(scaled, 1)
                    if e == 4 and not (isinstance(c, int) and c == 0):
                        finish(c - 1)

            moe(0)
            with dve.Fori(1, 2) as c:
                moe(c)
            with dve.Fori(2, NCH) as c:
                moe(c)
            finish(NCH - 1)

        @block.tensor
        def _(pe):
            mm = nc.tensor.matmul

            pe.wait_ge(w_ld, 16 * (2 * DLO + 1))
            for h in range(DHI):
                ins = mm(HG_PS[:, 64 * h:64 * h + 64], w_rows[:, h, :, :].rearrange("k r c -> k (r c)"), dft_sb[:, :],
                         start=h % 8 == 0, stop=h % 8 == 7, skip_group_check=True)
            ins.then_inc(weff_mm, 1)
            pe.wait_ge(hgw_ld, 16 * 4)
            mm(ST_PS[:, 0:P], center_sb[:, :], wg_bd[:, :], start=True, stop=True).then_inc(wgc_mm, 1)

            def tokenize(b):
                for pair in range(2):
                    pe.wait_ge(x_ld[pair][b % 2], 64 * (b // 2 + 1))
                    if pair == 0 and b:
                        pe.wait_ge(hT_ready, b)
                    for s in range(2):
                        for hop in range(2):
                            for hi in range(2):
                                first, last = (pair, s, hop) == (0, 0, 0), (pair, s, hop) == (1, 1, 1)
                                blk = 8 * hi + hop
                                win = x_sb[pair][b % 2][:, blk:blk + 8, s, :].rearrange("k (a j) v -> k j a v", a=2)
                                ins = mm(HT_PS[64 * hi:64 * hi + 64, :], w_eff[:, hop, 2 * pair + s, :], win,
                                         start=first, stop=last)
                    ins.then_inc(tok_done if pair else xa_used, 1)

            def h_and_gate(b):
                pe.wait_ge(hT_ready, b + 1)
                if b:
                    pe.wait_ge(h_ready, b)
                    pe.wait_ge(g_ready, b)
                for jj in range(4):
                    ins = mm(HG_PS[:, 256 * jj:256 * jj + 256], hT_sb[:, P * jj:P * jj + P], hg_rhs[:, :],
                             start=jj % 2 == 0, stop=jj % 2 == 1, skip_group_check=True)
                ins.then_inc(hg_done, 1)

            def transpose_s(b):
                pe.wait_ge(s_ready, b + 1)
                if b:
                    pe.wait_ge(sT_ready, b)
                for jj in range(4):
                    ins = nc.tensor.transpose(ST_PS[:, P * jj:P * jj + P], s_sb[:, P * jj:P * jj + P], hg_rhs[:, 0:P])
                ins.then_inc(st_done, 1)

            def project_o(b):
                pe.wait_ge(sT_ready, b + 1)
                if b:
                    pe.wait_ge(h2_ready, b)
                for jj in range(4):
                    ins = mm(WO_PS[:, P * jj:P * jj + P], sT_sb[:, P * jj:P * jj + P], wo_bd[:, :],
                             start=jj == 0, stop=jj == 3, skip_group_check=True)
                ins.then_inc(wo_done, 1)

            def transpose_x(b):
                pe.wait_ge(xl_ready, b + 1)
                pe.wait_ge(xh_ready, b + 1)
                if b:
                    pe.wait_ge(xT_ready, 2 * b)
                if b >= 2:
                    pe.wait_ge(cwT_ready, b - 1)
                for g in range(NG):
                    ins = nc.tensor.transpose(XT_PS[:, P * g:P * g + P], split_sb[:, g, :, :].rearrange("p k d -> p (k d)"),
                                              hg_rhs[:, 0:P])
                ins.then_inc(xt_done, 1)

            def gate_logits(b):
                pe.wait_ge(xT_ready, 2 * b + 2)
                if b:
                    pe.wait_ge(z_ready, b)
                for g in range(NG):
                    t = (NG * b + g) * P
                    ins = mm(LG_PS[:, 16 * g:16 * g + 16], xT_all[:, t:t + P], gw_r[:, :],
                             start=g == 0, stop=g == NG - 1, skip_group_check=True)
                ins.then_inc(lg_done, 1)

            def transpose_cw(b):
                pe.wait_ge(cw_ready, b + 1)
                pe.wait_ge(xT_ready, 2 * min(B, b + 2))
                for g in range(NG):
                    ins = nc.tensor.transpose(CT_PS[:, P * g:P * g + P],
                                              cw_sp[:, g, :, :].rearrange("p k e -> p (k e)"), ident_bf[:, :])
                ins.then_inc(ct_done, 1)

            pe.wait_ge(weff_ready, 16)
            tokenize(0)
            pe.wait_ge(hg_rhs_ready, 1)
            for b in range(B + 2):
                if b < B:
                    h_and_gate(b)
                if b >= 3:
                    transpose_cw(b - 3)
                if b + 1 < B:
                    tokenize(b + 1)
                if b == 0:
                    pe.wait_ge(wo_ready, 1)
                if b < B:
                    transpose_s(b)
                if 1 <= b <= B:
                    transpose_x(b - 1)
                if b < B:
                    project_o(b)
                if b == 1:
                    pe.wait_ge(gw_ready, 1)
                if 1 <= b <= B:
                    gate_logits(b - 1)
            transpose_cw(B - 1)

            def hidden(c, e):
                n = E * c + e
                if isinstance(c, int) and c == 0 and e < 4:
                    if e == 0:
                        pe.wait_ge(g_ready, B)
                        pe.wait_ge(h_ready, B)
                        pe.wait_ge(xT_ready, 2 * B)
                        pe.wait_ge(cwT_ready, B)
                        pe.wait_ge(w1_ready, 4)
                else:
                    pe.wait_ge(gelu_done, n - 3)
                xs = xT_all[:, bass.ts(c, CH)]
                mm(A_PS[e % 4], w1_hi[:, e, :], xs, start=True, stop=False)
                mm(A_PS[e % 4], w1_lo[:, e, :], xs, start=False, stop=True).then_inc(mm1_done, 1)

            def broadcast(c, e):
                n = E * c + e
                if isinstance(c, int) and c == 0 and e < 2:
                    if e == 0:
                        pe.wait_ge(sT_ready, B)
                        pe.wait_ge(h2_ready, B)
                        pe.wait_ge(sel_ready, 1)
                        pe.wait_ge(b2_ready, 1)
                else:
                    pe.wait_ge(scaled, n - 1)
                mm(B_PS[e % 2], sel_sb[:, e, :], cwT_all[:, bass.ts(c, CH)], start=True, stop=True).then_inc(bc_done, 1)

            def output_bias(c):
                if isinstance(c, int) and c == 0:
                    pe.wait_ge(w2_ld, 16)
                    pe.wait_ge(hT_ready, B)
                else:
                    pe.wait_ge(acc_ready, c)
                cs = cwT_all[:, bass.ts(c, CH)]
                for k in range(2):
                    mm(ACC_PS[:, :], b2_sp[:, 2 * k:2 * k + 2, :].rearrange("k a d -> k (a d)"), cs,
                       start=k == 0, stop=False, skip_group_check=True)

            def project_pair(c, k):
                for i in range(2):
                    e = 2 * k + i
                    pe.wait_ge(scaled, E * c + e + 1)
                    ins = mm(ACC_PS[64 * i:64 * i + 64, :], w2_sb[:, e, :], act_sb[:, e % 4, :],
                             start=False, stop=k == 3, skip_group_check=True)
                    ins.then_inc(mm2_done, 1)
                if k == 3:
                    pe.wait_ge(mm2_done, E * c + E)
                    pe.sem_inc(acc_done, 1)

            def transpose_out(c):
                pe.wait_ge(acc_ready, c + 1)
                if isinstance(c, int) and c == 0:
                    pe.wait_ge(z_ready, B)
                else:
                    pe.wait_ge(y_ready, c)
                for jj in range(4):
                    ins = nc.tensor.transpose(OT_PS[:, P * jj:P * jj + P], acc_sb[:, P * jj:P * jj + P], hg_rhs[:, 0:P])
                ins.then_inc(ot_done, 1)

            def moe(c):
                first = isinstance(c, int) and c == 0
                for k in range(4):
                    for i in range(2):
                        hidden(c, 2 * k + i)
                    for i in range(2):
                        broadcast(c, 2 * k + i)
                    if k == 0:
                        if not first:
                            project_pair(c - 1, 3)
                    else:
                        if k == 1:
                            output_bias(c)
                        project_pair(c, k - 1)
                        if k == 1 and not first:
                            transpose_out(c - 1)

            moe(0)
            moe(1)
            with pe.Fori(2, NCH) as c:
                moe(c)
            project_pair(NCH - 1, 3)
            transpose_out(NCH - 1)


_INS = {"x": "x", "W": "L0_tok_W", "wg": "L0_attn_wg", "wo": "L0_attn_wo", "gn_bias": "L0_attn_gn_bias",
        "attn_bias": "L0_attn_bias", "gate_w": "L0_ffn_gate_w", "gate_b": "L0_ffn_gate_b", "W1": "L0_ffn_W1",
        "b1": "L0_ffn_b1", "W2": "L0_ffn_W2", "b2": "L0_ffn_b2"}


def _constants(np):
    f, p = np.arange(NF)[:, None], np.arange(WIN)[None, :]
    angle = 2.0 * np.pi * ((f * p) % WIN) / WIN
    table = np.concatenate([np.cos(angle), -np.sin(angle)]) / np.sqrt(WIN)
    half = np.eye(2)
    return {
        "dft": np.kron(np.eye(DLO), table).astype(np.float32),
        "ident": np.eye(P, dtype=np.float32),
        "center": np.kron(half, np.eye(D) - 1.0 / D).astype(np.float32),
        "rank": (E - np.arange(E, dtype=np.float32))[None, :],
        "sel": np.tile(np.repeat(np.eye(E, dtype=np.float32)[:, :, None], P, axis=2), (NSPLIT, 1, 1)),
    }


def kernel(**inputs):
    import numpy as np
    import concourse.bacc as bacc
    from concourse.bass_utils import run_bass_kernel_spmd

    nc = bacc.Bacc("TRN2", target_bir_lowering=False, num_devices=1)
    data = {k: np.ascontiguousarray(inputs[v]) for k, v in _INS.items()}
    data.update(_constants(np))
    arrays, args = {}, {}
    for name, a in data.items():
        arrays[f"in_{name}"] = a
        args[name] = nc.dram_tensor(f"in_{name}", a.shape, mybir.dt.from_np(a.dtype), kind="ExternalInput").ap()
    out = nc.dram_tensor("out", (B, V * NWIN, D), F32, kind="ExternalOutput").ap()
    vit_layer(nc, out=out, **args)
    r = run_bass_kernel_spmd(nc, [arrays], core_ids=[0])
    return r.results[0]["out"]
```

```python
from contextlib import ExitStack

import concourse.bass as bass
from concourse import mybir

ALU = mybir.AluOpType
ACT = mybir.ActivationFunctionType
F32 = mybir.dt.float32
F32R = mybir.dt.float32r
BF16 = mybir.dt.bfloat16
AX_X = mybir.AxisListType.X

B, C, T, V = 4, 64, 128, 64
WIN, HOP = 16, 8
NF = WIN // 2 + 1
G = 2 * NF
NWIN = T // HOP
D = 64
E, H = 8, 128
EPS = 1e-5
P = 128
DLO = 4
DHI = D // DLO
NG = 8
NCH = 2 * B
CH = 512
PAIRS = E // 2
WARM = 14
RS = 2


def vit_layer(nc, x, W, wg, wo, gn_bias, attn_bias, gate_w, gate_b, W1, b1, W2, b2, dft, ident, center, rank, sel, out):
    ctx = ExitStack()
    with ctx:
        def sb(name, shape, dt=F32):
            return ctx.enter_context(nc.sbuf_tensor(name, shape, dt))

        def sem(name):
            return ctx.enter_context(nc.semaphore(name))

        x_sb = [sb(f"x_{par}", [P, NWIN + 1, 4, V]) for par in range(2)]
        warm = sb("warm", [P, 512], BF16)
        w_rows = sb("w_rows", [DLO * G, DHI, 2, C])
        dft_sb = sb("dft_sb", [DLO * G, DLO * WIN])
        w_eff = sb("w_eff", [P, 2, 4, D])
        ident_sb = sb("ident_sb", [P, P])
        center_sb = sb("center_sb", [P, P])
        wg_bd = sb("wg_bd", [P, P])
        wgc_bd = sb("wgc_bd", [P, P])
        wo_bd = sb("wo_bd", [P, P])
        gnb = sb("gnb", [P, 1])
        bias_b = sb("bias_b", [P, D])
        gate_b_b = sb("gate_b_b", [P, E])
        rank_b = sb("rank_b", [P, E])
        gw_raw = sb("gw_raw", [P, E])
        gw_r = sb("gw_r", [P, RS * E], F32R)
        w1_raw = sb("w1_raw", [P, E, H])
        w1_hi = sb("w1_hi", [P, E, H], F32R)
        w1_lo = sb("w1_lo", [P, E, H], F32R)
        w2_sb = sb("w2_sb", [P, E, D])
        b1_sb = sb("b1_sb", [P, E])
        b2_sb = sb("b2_sb", [P, PAIRS])
        sel_f = sb("sel_f", [RS * E, PAIRS, P])
        sel_sb = sb("sel_sb", [P, PAIRS, P], F32R)
        expo = sb("expo", [P, NG])

        hT_sb = sb("hT_sb", [P, CH])
        h_sb = sb("h_sb", [P, NG, D])
        hb_sb = sb("hb_sb", [P, NG, D])
        g_sb = sb("g_sb", [P, NG * D])
        th_sb = sb("th_sb", [P, NG * D])
        s_sb = sb("s_sb", [P, NG * D])
        sT_sb = sb("sT_sb", [P, CH])
        st1 = sb("st1", [P, NG, 6])
        st2 = sb("st2", [P, NG, 6])
        sm1 = sb("sm1", [P, 6, NG])
        sm2 = sb("sm2", [P, 6, NG])
        h2_all = sb("h2_all", [P, NCH * 4, D])
        xc_sb = sb("xc_sb", [P, NG, D])
        xn_sb = sb("xn_sb", [P, NG, D])
        split_sb = sb("split_sb", [P, NG, RS, D])
        xT_all = sb("xT_all", [P, NCH * CH], F32R)
        lz = sb("lz", [P, 6, 2 * NG, E])
        lm = sb("lm", [P, 7, 2 * NG])
        table_sb = sb("table_sb", [P, 1])
        cw = sb("cw", [P, 2 * NG, E])
        cw_sp = sb("cw_sp", [P, 2 * NG, RS, E])
        cwT_all = sb("cwT_all", [P, NCH * CH], F32R)
        act_sb = sb("act_sb", [P, 4, CH])
        cwb_sb = sb("cwb_sb", [P, 2, CH])
        yw_sb = sb("yw_sb", [P, 2, CH])
        acc_sb = sb("acc_sb", [P, CH])
        fin_sb = sb("fin_sb", [P, CH])
        y_sb = sb("y_sb", [P, 4, D])
        o_sb = sb("o_sb", [P, 4, D])

        bank = [ctx.enter_context(nc.psum_tensor(f"bank{i}", [P, 512], F32)) for i in range(8)]
        HT_PS, HP_PS, GP_PS, ST_PS, WO_PS, LG_PS = (bank[i] for i in (0, 1, 2, 3, 4, 7))
        XT_PS = [bank[5], bank[6]]
        GATE_PS = [GP_PS] * 3 + [bank[6]]
        A_EARLY, A_LATE = [bank[0], bank[1], bank[0], bank[1]], [bank[4], bank[5], bank[0], bank[1]]
        CT_PS = [bank[5] if c < 4 else bank[7] for c in range(NCH)]
        CB_PS, Y_PS, OT_EARLY, OT_LATE = bank[2], [bank[3], bank[6]], bank[4], bank[7]

        x_first = sem("x_first")
        x_ld = [sem(f"x_ld_{par}") for par in range(2)]
        w_ld, id_ld, wg_ld, wo_ld, vec_ld, w1_ld, w2_ld, sel_ld = (
            sem(n) for n in "w_ld id_ld wg_ld wo_ld vec_ld w1_ld w2_ld sel_ld".split())
        warm_set, zeroed, w_twice = sem("warm_set"), sem("zeroed"), sem("w_twice")
        weff_mm, weff_ready, wgc_mm, wgc_ready = (sem(n) for n in "weff_mm weff_ready wgc_mm wgc_ready".split())
        wo_ready, gw_ready, w1_ready, sel_ready = (sem(n) for n in "wo_ready gw_ready w1_ready sel_ready".split())
        tok_done, hT_ready, hp_done, hg_done, h_ready, var1, rstd1, g_ready, tanh_done = (
            sem(n) for n in "tok_done hT_ready hp_done hg_done h_ready var1 rstd1 g_ready tanh_done".split())
        s_ready, st_done, sT_ready, wo_done, hb_ready, h2_ready, var2, rstd2, xn_ready, xh_ready, xl_ready = (
            sem(n) for n in "s_ready st_done sT_ready wo_done hb_ready h2_ready var2 rstd2 xn_ready xh_ready xl_ready".split())
        xt_done, xT_ready, lg_done, z_ready, exp_done, cw_ready, ct_done, cwT_ready = (
            sem(n) for n in "xt_done xT_ready lg_done z_ready exp_done cw_ready ct_done cwT_ready".split())
        mm1_done, gelu_done, cb_done, cwb_ready, mm2_done, weighted, added, ot_done, y1_done, y_ready, out_st = (
            sem(n) for n in "mm1_done gelu_done cb_done cwb_ready mm2_done weighted added ot_done y1_done y_ready out_st".split())
        dve_step = sem("dve_step")

        def grp(ap):
            return ap.rearrange("p (j h d) -> p j h d", j=4, h=2)

        def is_first(c):
            return isinstance(c, int) and c == 0

        def move_w_eff(copy, half):
            rows = slice(64 * half, 64 * half + 64)
            for hop in range(2):
                p0 = HOP * hop + 4 * half
                for n, b in enumerate((HP_PS, GP_PS)):
                    src = b[rows, :].rearrange("c (h l p) -> c p l h", l=DLO, p=WIN)[:, p0:p0 + 4, :, :]
                    dst = w_eff[rows, hop, :, :].rearrange("c s (l m h) -> c s l m h", l=DLO, m=2)[:, :, :, n, :]
                    copy(dst, src).then_inc(weff_ready, 1)

        block = ctx.enter_context(nc.Block())

        @block.sync
        def _(sp):
            xv = x.rearrange("b c (m h s) v -> b h c m s v", h=2, s=4)

            def load_edge(b, done):
                for half in range(2):
                    sp.dma_start(x_sb[b % 2][64 * half:64 * half + 64, NWIN, :, :],
                                 x[b, :, T - 1:T, :].to_broadcast([C, 4, V])).then_inc(done, 16)

            def load_x(b, steps, done):
                for half in range(2):
                    sp.dma_start(x_sb[b % 2][64 * half:64 * half + 64, 0:NWIN, steps, :], xv[b, half, :, :, steps, :]
                                 ).then_inc(done, 16)

            wv = W.rearrange("(l h) (g c) -> l g h c", l=DLO, c=C)
            for l in (0, 2):
                sp.dma_start(w_rows[G * l:G * l + G, :, 0, :], wv[l]).then_inc(w_ld, 16)
            load_x(0, slice(0, 2), x_first)
            load_edge(0, x_first)
            load_x(0, slice(2, 4), x_ld[0])
            sp.wait_ge(zeroed, 2)
            for hi in range(2):
                sp.dma_start(wo_bd[64 * hi:64 * hi + 64, 64 * hi:64 * hi + 64], wo).then_inc(wo_ld, 16)
                sp.dma_start(gnb[64 * hi:64 * hi + 64, :], gn_bias.rearrange("(d o) -> d o", o=1)).then_inc(wo_ld, 16)
            load_x(1, slice(0, 4), x_ld[1])
            load_edge(1, x_ld[1])
            sp.dma_start(bias_b[:, :], attn_bias.rearrange("(o d) -> o d", o=1).to_broadcast([P, D])).then_inc(vec_ld, 16)
            sp.dma_start(gate_b_b[:, :], gate_b.rearrange("(o e) -> o e", o=1).to_broadcast([P, E])).then_inc(vec_ld, 16)
            sp.dma_start(rank_b[:, :], rank.to_broadcast([P, E])).then_inc(vec_ld, 16)
            sp.dma_start(b1_sb[:, :], b1.rearrange("e h -> h e"), allow_slow_non_contiguous=True).then_inc(vec_ld, 16)
            b2v = b2.rearrange("(k i) d -> i d k", i=2)
            for i in range(2):
                sp.dma_start(gw_raw[64 * i:64 * i + 64, :], gate_w).then_inc(vec_ld, 16)
                sp.dma_start(b2_sb[64 * i:64 * i + 64, :], b2v[i], allow_slow_non_contiguous=True).then_inc(vec_ld, 16)
            for hi in range(2):
                sp.dma_start(w1_raw[64 * hi:64 * hi + 64, :, :], W1.rearrange("e d h -> d e h")).then_inc(w1_ld, 16)
            for b in (2, 3):
                sp.wait_ge(tok_done, b - 1)
                load_x(b, slice(0, 4), x_ld[b % 2])
                load_edge(b, x_ld[b % 2])
                if b == 2:
                    sp.dma_start(sel_f[:, :, :], sel).then_inc(sel_ld, 16)
                    sp.dma_start(w2_sb[:, :, :], W2.rearrange("e h d -> h e d")).then_inc(w2_ld, 16)
            ov = out.rearrange("b (v h k j) d -> b h k v (j d)", h=2, k=2, j=4)
            with sp.Fori(0, B) as b:
                for hi in range(2):
                    sp.wait_ge(y_ready, 2 * b + hi + 1)
                    for j4 in range(2):
                        sp.dma_start(ov[b, hi, j4, :, :], o_sb[64 * j4:64 * j4 + 64, :, :].rearrange("v j d -> v (j d)")
                                     ).then_inc(out_st, 16)
            sp.wait_ge(out_st, 32 * NCH)

        @block.gpsimd
        def _(pool):
            for t in (wg_bd, wo_bd):
                nc.gpsimd.memset(t[:, :], 0.0).then_inc(zeroed, 1)
            nc.gpsimd.memset(expo[:, :], -0.5).then_inc(zeroed, 1)
            nc.gpsimd.memset(sel_sb[:, :, :].bitcast(F32), 0.0).then_inc(zeroed, 1)
            nc.gpsimd.memset(cwT_all[:, :].bitcast(F32), 0.0).then_inc(zeroed, 1)
            pool.wait_ge(zeroed, 3)
            pool.wait_ge(vec_ld, 16 * 8)

            def add_bias(b):
                pool.wait_ge(h_ready, b + 1)
                if b:
                    pool.wait_ge(h2_ready, b)
                nc.gpsimd.tensor_tensor(hb_sb[:, :, :], h_sb[:, :, :], bias_b[:, None, :].to_broadcast([P, NG, D]),
                                        ALU.add).then_inc(hb_ready, 1)

            def rsqrt(sm, ready, done, b):
                pool.wait_ge(ready, b + 1)
                nc.gpsimd.tensor_tensor(sm[:, 5, :], sm[:, 4, :], expo[:, :], ALU.pow).then_inc(done, 1)

            def low_part(b):
                pool.wait_ge(xn_ready, b + 1)
                pool.wait_ge(xh_ready, b + 1)
                nc.gpsimd.tensor_tensor(split_sb[:, :, 1, :], xn_sb[:, :, :], split_sb[:, :, 0, :], ALU.subtract
                                        ).then_inc(xl_ready, 1)

            def accumulate(c, k):
                pool.wait_ge(weighted, PAIRS * c + k + 1)
                dst = acc_sb if k < PAIRS - 1 else fin_sb
                if k > 1:
                    pool.wait_ge(added, 3 * c + k - 1)
                if k == PAIRS - 1 and not is_first(c):
                    pool.wait_ge(ot_done, c)
                nc.gpsimd.tensor_tensor(dst[:, :], yw_sb[:, k % 2, :], acc_sb[:, :], ALU.add).then_inc(added, 1)

            for b in range(3):
                if b:
                    rsqrt(sm2, var2, rstd2, b - 1)
                rsqrt(sm1, var1, rstd1, b)
                if b:
                    low_part(b - 1)
                add_bias(b)
            rsqrt(sm1, var1, rstd1, 3)
            rsqrt(sm2, var2, rstd2, 2)
            add_bias(3)
            accumulate(0, 1)
            low_part(2)
            accumulate(0, 2)
            accumulate(0, 3)
            rsqrt(sm2, var2, rstd2, 3)
            accumulate(1, 1)
            accumulate(1, 2)
            low_part(3)
            accumulate(1, 3)
            for c in range(2, 4):
                for k in range(1, PAIRS):
                    accumulate(c, k)
            with pool.Fori(4, NCH) as c:
                for k in range(1, PAIRS):
                    accumulate(c, k)

        @block.scalar
        def _(act):
            act.dma_start(dft_sb[:, :], dft).then_inc(w_ld, 16)
            wv = W.rearrange("(l h) (g c) -> l g h c", l=DLO, c=C)
            for l in (1, 3):
                act.dma_start(w_rows[G * l:G * l + G, :, 0, :], wv[l]).then_inc(w_ld, 16)
            act.dma_start(center_sb[:, :], center).then_inc(wg_ld, 16)
            act.wait_ge(zeroed, 3)
            for hi in range(2):
                act.dma_start(wg_bd[64 * hi:64 * hi + 64, 64 * hi:64 * hi + 64], wg).then_inc(wg_ld, 16)
            act.dma_start(ident_sb[:, :], ident).then_inc(id_ld, 16)

            act.wait_ge(weff_mm, 1)
            move_w_eff(nc.scalar.copy, 1)

            def evac_hT(b):
                act.wait_ge(tok_done, b + 1)
                if b:
                    act.wait_ge(hg_done, b)
                nc.scalar.activation(hT_sb[:, :], HT_PS[:, :], ACT.Copy).then_inc(hT_ready, 1)

            def evac_h(b):
                act.wait_ge(hp_done, b + 1)
                if b:
                    act.wait_ge(var1, b)
                    act.wait_ge(hb_ready, b)
                nc.scalar.activation(h_sb[:, :, :].rearrange("p g d -> p (g d)"), HP_PS[:, :], ACT.Copy).then_inc(h_ready, 1)

            def tanh(b):
                act.wait_ge(g_ready, b + 1)
                if b:
                    act.wait_ge(s_ready, b)
                nc.scalar.activation(th_sb[:, :], g_sb[:, :], ACT.Tanh, scale=0.5).then_inc(tanh_done, 1)

            def evac_sT(b):
                act.wait_ge(st_done, b + 1)
                if b:
                    act.wait_ge(wo_done, b)
                nc.scalar.activation(sT_sb[:, :], (WO_PS if b == 3 else ST_PS)[:, :], ACT.Copy).then_inc(sT_ready, 1)

            def high_part(b):
                act.wait_ge(xn_ready, b + 1)
                if b:
                    act.wait_ge(xt_done, 2 * b)
                nc.scalar.activation(split_sb[:, :, 0, :].bitcast(F32R), xn_sb[:, :, :], ACT.Copy).then_inc(xh_ready, 1)

            def evac_xT(b, half):
                act.wait_ge(xt_done, 2 * b + half + 1)
                c = 2 * b + half
                nc.scalar.activation(xT_all[:, c * CH:(c + 1) * CH], XT_PS[0 if b >= 2 else half][:, :], ACT.Copy
                                     ).then_inc(xT_ready, 1)

            def exp(g0, n, count):
                act.wait_ge(z_ready, count)
                nc.scalar.activation(lz[:, 2, g0:g0 + n, :], lz[:, 1, g0:g0 + n, :], ACT.Exp).then_inc(exp_done, 1)

            def evac_cwT(c):
                act.wait_ge(ct_done, c + 1)
                if c == 0:
                    act.wait_ge(zeroed, 5)
                nc.scalar.activation(cwT_all[0:RS * E, c * CH:(c + 1) * CH], CT_PS[c][0:RS * E, :], ACT.Copy
                                     ).then_inc(cwT_ready, 1)

            def moe(c, k, A):
                p = PAIRS * c + k
                for i in range(2):
                    e = 2 * k + i
                    act.wait_ge(mm1_done, E * c + e + 1)
                    if i == 0 and not (is_first(c) and k < 2):
                        act.wait_ge(mm2_done, p - 1)
                    nc.scalar.activation(act_sb[:, e % 4, :], A[e % 4][:, :], ACT.Gelu, bias=b1_sb[:, e:e + 1]
                                         ).then_inc(gelu_done, 1)
                act.wait_ge(cb_done, p + 1)
                if not (is_first(c) and k < 2):
                    act.wait_ge(weighted, p - 1)
                nc.scalar.activation(cwb_sb[:, k % 2, :], CB_PS[:, :], ACT.Copy).then_inc(cwb_ready, 1)

            evac_hT(0)
            for b in range(3):
                evac_h(b)
                if b:
                    high_part(b - 1)
                if b == 2:
                    exp(0, NG, 1)
                tanh(b)
                if b:
                    evac_hT(b + 1)
                    evac_sT(b)
                    evac_xT(b - 1, 0)
                    evac_xT(b - 1, 1)
                else:
                    evac_sT(b)
                    evac_hT(b + 1)
            evac_h(3)
            exp(NG, NG, 2)
            act.wait_ge(vec_ld, 16 * 8)
            nc.scalar.activation(table_sb[:, :], b1_sb[:, 0:1], ACT.Gelu)
            evac_cwT(0)
            moe(0, 0, A_EARLY)
            evac_cwT(1)
            moe(0, 1, A_EARLY)
            tanh(3)
            moe(0, 2, A_EARLY)
            evac_sT(3)
            high_part(2)
            moe(0, 3, A_EARLY)
            moe(1, 0, A_EARLY)
            evac_xT(2, 0)
            moe(1, 1, A_EARLY)
            evac_xT(2, 1)
            moe(1, 2, A_EARLY)
            moe(1, 3, A_EARLY)
            evac_cwT(2)
            moe(2, 0, A_EARLY)
            evac_cwT(3)
            high_part(3)
            moe(2, 1, A_EARLY)
            evac_xT(3, 0)
            moe(2, 2, A_EARLY)
            evac_xT(3, 1)
            moe(2, 3, A_EARLY)
            moe(3, 0, A_LATE)
            exp(0, 2 * NG, 3)
            moe(3, 1, A_LATE)
            moe(3, 2, A_LATE)
            moe(3, 3, A_LATE)
            evac_cwT(4)
            moe(4, 0, A_LATE)
            evac_cwT(5)
            moe(4, 1, A_LATE)
            evac_cwT(6)
            moe(4, 2, A_LATE)
            moe(4, 3, A_LATE)
            evac_cwT(7)
            with act.Fori(5, NCH) as c:
                for k in range(PAIRS):
                    moe(c, k, A_LATE)

        @block.vector
        def _(dve):
            steps = [0]

            def link(ins):
                steps[0] += 1
                ins.then_inc(dve_step, 1)
                dve.wait_ge(dve_step, steps[0])

            nc.vector.memset(warm[:, :], 0.0).then_inc(warm_set, 1)
            dve.wait_ge(w_ld, 16 * (DLO + 1))
            nc.vector.tensor_copy(w_rows[:, :, 1, :], w_rows[:, :, 0, :]).then_inc(w_twice, 1)
            dve.wait_ge(weff_mm, 1)
            move_w_eff(nc.vector.tensor_copy, 0)
            dve.wait_ge(wgc_mm, 1)
            nc.vector.tensor_copy(wgc_bd[:, :], ST_PS[:, 0:P]).then_inc(wgc_ready, 1)
            dve.wait_ge(wo_ld, 16 * 4)
            nc.vector.tensor_scalar(wo_bd[:, :], wo_bd[:, :], gnb[:, 0:1], 0.5, ALU.mult, ALU.mult).then_inc(wo_ready, 1)

            def prep_gate():
                dve.wait_ge(vec_ld, 16 * 8)
                link(nc.vector.tensor_copy(gw_r[:, 0:E], gw_raw[:, :]))
                nc.vector.tensor_tensor(gw_r[:, E:2 * E], gw_raw[:, :], gw_r[:, 0:E].bitcast(F32), ALU.subtract
                                        ).then_inc(gw_ready, 1)

            def prep_w1(part):
                es = slice(4 * part, 4 * part + 4)
                dve.wait_ge(w1_ld, 32)
                link(nc.vector.tensor_copy(w1_hi[:, es, :], w1_raw[:, es, :]))
                nc.vector.tensor_tensor(w1_lo[:, es, :], w1_raw[:, es, :], w1_hi[:, es, :].bitcast(F32), ALU.subtract
                                        ).then_inc(w1_ready, 1)

            def prep_sel():
                dve.wait_ge(sel_ld, 16)
                dve.wait_ge(zeroed, 4)
                nc.vector.tensor_copy(sel_sb[0:RS * E, :, :], sel_f[:, :, :]).then_inc(sel_ready, 1)

            def variance(src, st, sm, done, mean):
                for g in range(NG):
                    nc.vector.bn_stats(st[:, g, :], src[:, g, :]).then_inc(dve_step, 1)
                steps[0] += NG
                dve.wait_ge(dve_step, steps[0])
                me, m2e, mo, m2o = (st[:, :, k] for k in (1, 2, 4, 5))
                nc.vector.tensor_tensor(sm[:, 1, :], m2e, m2o, ALU.add).then_inc(dve_step, 1)
                if mean:
                    nc.vector.tensor_tensor(sm[:, 2, :], me, mo, ALU.add).then_inc(dve_step, 1)
                nc.vector.tensor_tensor(sm[:, 0, :], me, mo, ALU.subtract).then_inc(dve_step, 1)
                steps[0] += 3 if mean else 2
                dve.wait_ge(dve_step, steps[0])
                link(nc.vector.tensor_tensor(sm[:, 3, :], sm[:, 0, :], sm[:, 0, :], ALU.mult))
                link(nc.vector.scalar_tensor_tensor(sm[:, 0, :], sm[:, 3, :], D / 4.0, sm[:, 1, :], ALU.mult, ALU.add))
                nc.vector.tensor_scalar(sm[:, 4, :], sm[:, 0, :], 1.0 / D, EPS, ALU.mult, ALU.add).then_inc(done, 1)
                if mean:
                    nc.vector.tensor_scalar(sm[:, 3, :], sm[:, 2, :], 0.5, None, ALU.mult).then_inc(dve_step, 1)
                    steps[0] += 1

            def ln1_stats(b):
                dve.wait_ge(h_ready, b + 1)
                variance(h_sb, st1, sm1, var1, False)

            def scale_g(b):
                dve.wait_ge(rstd1, b + 1)
                dve.wait_ge(hg_done, b + 1)
                nc.vector.tensor_tensor(g_sb[:, :].rearrange("p (g d) -> p g d", g=NG),
                                        GATE_PS[b][:, :].rearrange("p (g d) -> p g d", g=NG),
                                        sm1[:, 5, :, None].to_broadcast([P, NG, D]), ALU.mult).then_inc(g_ready, 1)

            def silu(b):
                dve.wait_ge(tanh_done, b + 1)
                if b:
                    dve.wait_ge(st_done, b)
                nc.vector.scalar_tensor_tensor(s_sb[:, :], th_sb[:, :], 1.0, g_sb[:, :], ALU.add, ALU.mult
                                               ).then_inc(s_ready, 1)

            def residual(b):
                dve.wait_ge(wo_done, b + 1)
                dve.wait_ge(hb_ready, b + 1)
                nc.vector.tensor_tensor(h2_all[:, 8 * b:8 * b + 8, :].rearrange("p (h j) d -> p j h d", h=2),
                                        grp(WO_PS[:, :]), grp(hb_sb[:, :, :].rearrange("p g d -> p (g d)")),
                                        ALU.add).then_inc(h2_ready, 1)

            def ln2_stats(b):
                dve.wait_ge(h2_ready, b + 1)
                variance(h2_all[:, 8 * b:8 * b + 8, :], st2, sm2, var2, True)

            def ln2_center(b):
                dve.wait_ge(dve_step, steps[0])
                link(nc.vector.tensor_tensor(xc_sb[:, :, :], h2_all[:, 8 * b:8 * b + 8, :],
                                             sm2[:, 3, :, None].to_broadcast([P, NG, D]), ALU.subtract))

            def ln2_scale(b):
                dve.wait_ge(rstd2, b + 1)
                if b:
                    dve.wait_ge(xh_ready, b)
                    dve.wait_ge(xl_ready, b)
                nc.vector.tensor_tensor(xn_sb[:, :, :], xc_sb[:, :, :], sm2[:, 5, :, None].to_broadcast([P, NG, D]),
                                        ALU.mult).then_inc(xn_ready, 1)

            def logits(g0, n, count):
                dve.wait_ge(lg_done, count)
                lg = LG_PS[:, 16 * g0:16 * (g0 + n)].rearrange("p (g k e) -> p g k e", g=n, k=2)
                gs, bc = slice(g0, g0 + n), [P, n, E]
                link(nc.vector.tensor_tensor(lz[:, 0, gs, :], lg[:, :, 0, :], gate_b_b[:, None, :].to_broadcast(bc), ALU.add))
                link(nc.vector.tensor_tensor(lz[:, 3, gs, :], lg[:, :, 1, :], lz[:, 0, gs, :], ALU.add))
                link(nc.vector.tensor_reduce(lm[:, 0, gs], lz[:, 3, gs, :], AX_X, ALU.max))
                nc.vector.tensor_tensor(lz[:, 1, gs, :], lz[:, 3, gs, :], lm[:, 0, gs, None].to_broadcast(bc),
                                        ALU.subtract).then_inc(z_ready, 1)

            def route_first(g0, n, count):
                gs, bc = slice(g0, g0 + n), [P, n, E]
                z, ex, key, hot1 = (lz[:, k, gs, :] for k in (1, 2, 3, 4))
                dve.wait_ge(z_ready, count)
                link(nc.vector.scalar_tensor_tensor(key, z, 0.0, rank_b[:, None, :].to_broadcast(bc), ALU.is_equal, ALU.mult))
                link(nc.vector.tensor_reduce(lm[:, 3, gs], key, AX_X, ALU.max))
                link(nc.vector.tensor_tensor(hot1, key, lm[:, 3, gs, None].to_broadcast(bc), ALU.is_equal))
                dve.wait_ge(exp_done, count)
                link(nc.vector.tensor_reduce(lm[:, 1, gs], ex, AX_X, ALU.add))
                link(nc.vector.reciprocal(lm[:, 2, gs], lm[:, 1, gs]))

            def route_second(g0, n):
                gs, bc = slice(g0, g0 + n), [P, n, E]
                ex, key, hot1, rest = (lz[:, k, gs, :] for k in (2, 3, 4, 5))
                link(nc.vector.scalar_tensor_tensor(rest, hot1, -2.0, ex, ALU.mult, ALU.add))
                link(nc.vector.tensor_reduce(lm[:, 4, gs], rest, AX_X, ALU.max))
                link(nc.vector.tensor_tensor(key, rest, lm[:, 4, gs, None].to_broadcast(bc), ALU.is_equal))
                link(nc.vector.tensor_tensor(key, key, rank_b[:, None, :].to_broadcast(bc), ALU.mult))
                link(nc.vector.tensor_reduce(lm[:, 5, gs], key, AX_X, ALU.max))
                link(nc.vector.tensor_tensor(rest, key, lm[:, 5, gs, None].to_broadcast(bc), ALU.is_equal))

            def route_weights(g0, n, ct):
                gs, bc = slice(g0, g0 + n), [P, n, E]
                ex, key, hot1, hot2 = (lz[:, k, gs, :] for k in (2, 3, 4, 5))
                link(nc.vector.tensor_tensor(key, hot1, hot2, ALU.add))
                link(nc.vector.tensor_tensor(key, ex, key, ALU.mult))
                link(nc.vector.tensor_tensor(cw[:, gs, :], key, lm[:, 2, gs, None].to_broadcast(bc), ALU.mult))
                if ct:
                    dve.wait_ge(ct_done, ct)
                link(nc.vector.tensor_copy(cw_sp[:, gs, 0, :].bitcast(F32R), cw[:, gs, :]))
                nc.vector.tensor_tensor(cw_sp[:, gs, 1, :], cw[:, gs, :], cw_sp[:, gs, 0, :], ALU.subtract
                                        ).then_inc(cw_ready, 1)

            def weigh(c, k):
                p = PAIRS * c + k
                dve.wait_ge(mm2_done, p + 1)
                dve.wait_ge(cwb_ready, p + 1)
                if k == 0:
                    if not is_first(c):
                        dve.wait_ge(added, 3 * c)
                elif not (is_first(c) and k < 3):
                    if k == 3:
                        dve.wait_ge(added, 3 * c + 1)
                    else:
                        dve.wait_ge(added, 3 * c)
                nc.vector.scalar_tensor_tensor((acc_sb[:, :] if k == 0 else yw_sb[:, k % 2, :]), Y_PS[k % 2][:, :],
                                               b2_sb[:, k:k + 1], cwb_sb[:, k % 2, :], ALU.add, ALU.mult
                                               ).then_inc(weighted, 1)

            def finish(c, OT_PS):
                dve.wait_ge(ot_done, c + 1)
                ot = OT_PS[:, :].rearrange("p (j k d) -> p j k d", j=4, k=2)
                nc.vector.tensor_tensor(y_sb[:, :, :], ot[:, :, 0, :], h2_all[:, bass.ts(c, 4), :], ALU.add
                                        ).then_inc(y1_done, 1)
                dve.wait_ge(y1_done, c + 1)
                if not is_first(c):
                    dve.wait_ge(out_st, 32 * c)
                nc.vector.tensor_tensor(o_sb[:, :, :], ot[:, :, 1, :], y_sb[:, :, :], ALU.add).then_inc(y_ready, 1)

            for b in range(3):
                if b:
                    residual(b - 1)
                    ln2_stats(b - 1)
                ln1_stats(b)
                if b:
                    if b == 2:
                        logits(0, NG, 1)
                    ln2_center(b - 1)
                    ln2_scale(b - 1)
                scale_g(b)
                if b == 0:
                    prep_gate()
                if b == 2:
                    route_first(0, NG, 1)
                silu(b)
                if b < 2:
                    prep_w1(b)
                else:
                    prep_sel()
                    route_second(0, NG)
                    route_weights(0, NG, 0)
            logits(NG, NG, 2)
            ln1_stats(3)
            residual(2)
            ln2_stats(2)
            scale_g(3)
            weigh(0, 0)
            silu(3)
            ln2_center(2)
            weigh(0, 1)
            ln2_scale(2)
            weigh(0, 2)
            route_first(NG, NG, 2)
            weigh(0, 3)
            route_second(NG, NG)
            residual(3)
            weigh(1, 0)
            ln2_stats(3)
            weigh(1, 1)
            route_weights(NG, NG, 2)
            finish(0, OT_EARLY)
            weigh(1, 2)
            ln2_center(3)
            ln2_scale(3)
            weigh(1, 3)
            weigh(2, 0)
            weigh(2, 1)
            finish(1, OT_EARLY)
            weigh(2, 2)
            logits(0, 2 * NG, 4)
            weigh(2, 3)
            route_first(0, NG, 3)
            weigh(3, 0)
            route_second(0, NG)
            route_weights(0, NG, 4)
            weigh(3, 1)
            route_first(NG, NG, 3)
            finish(2, OT_LATE)
            weigh(3, 2)
            route_second(NG, NG)
            weigh(3, 3)
            route_weights(NG, NG, 4)
            weigh(4, 0)
            weigh(4, 1)
            finish(3, OT_LATE)
            weigh(4, 2)
            weigh(4, 3)
            with dve.Fori(5, NCH) as c:
                weigh(c, 0)
                weigh(c, 1)
                finish(c - 1, OT_LATE)
                weigh(c, 2)
                weigh(c, 3)
            finish(NCH - 1, OT_LATE)

        @block.tensor
        def _(pe):
            mm = nc.tensor.matmul

            pe.wait_ge(warm_set, 1)
            def keep_warm(n, size=512):
                for _ in range(n):
                    mm(bank[7][:, 0:size], warm[:, 0:P], warm[:, 0:size], start=True, stop=True, skip_group_check=True)

            keep_warm(WARM)

            pe.wait_ge(w_ld, 16 * (DLO + 1))
            pe.wait_ge(w_twice, 1)
            for h in range(DHI):
                ins = mm((HP_PS, GP_PS)[h // 8][:, 64 * (h % 8):64 * (h % 8) + 64],
                         w_rows[:, h, :, :].rearrange("k r c -> k (r c)"), dft_sb[:, :],
                         start=h % 8 == 0, stop=h % 8 == 7, skip_group_check=True)
                if h < DHI - 1:
                    keep_warm(1, 128)
            ins.then_inc(weff_mm, 1)
            pe.wait_ge(wg_ld, 16 * 3)
            mm(ST_PS[:, 0:P], center_sb[:, :], wg_bd[:, :], start=True, stop=True).then_inc(wgc_mm, 1)

            def tokenize(b, steps=range(4)):
                if b == 0:
                    pe.wait_ge(x_first, 16 * 4)
                elif steps[0] == 0:
                    pe.wait_ge(x_ld[b % 2], (32, 64, 96, 128)[b])
                    pe.wait_ge(hT_ready, b)
                for s in steps:
                    if b == 0 and s == 2:
                        pe.wait_ge(x_ld[0], 32)
                    for hop in range(2):
                        for hi in range(2):
                            blk = 8 * hi + hop
                            win = x_sb[b % 2][:, blk:blk + 8, s, :].rearrange("k (a j) v -> k j a v", a=2)
                            ins = mm(HT_PS[64 * hi:64 * hi + 64, :], w_eff[:, hop, s, :], win,
                                     start=(s, hop) == (0, 0), stop=(s, hop) == (3, 1))
                if steps[-1] == 3:
                    ins.then_inc(tok_done, 1)

            def h_and_gate(b):
                pe.wait_ge(hT_ready, b + 1)
                if b:
                    pe.wait_ge(h_ready, b)
                    pe.wait_ge(g_ready, b)
                if b == 3:
                    pe.wait_ge(xT_ready, 4)
                for jj in range(4):
                    ins = nc.tensor.transpose(HP_PS[:, P * jj:P * jj + P], hT_sb[:, P * jj:P * jj + P], ident_sb[:, :])
                ins.then_inc(hp_done, 1)
                for jj in range(4):
                    ins = mm(GATE_PS[b][:, P * jj:P * jj + P], hT_sb[:, P * jj:P * jj + P], wgc_bd[:, :],
                             start=jj == 0, stop=jj == 3, skip_group_check=True)
                ins.then_inc(hg_done, 1)

            def transpose_s(b):
                pe.wait_ge(s_ready, b + 1)
                if b:
                    pe.wait_ge(sT_ready, b)
                if b == 3:
                    pe.wait_ge(h2_ready, 3)
                for jj in range(4):
                    ins = nc.tensor.transpose((WO_PS if b == 3 else ST_PS)[:, P * jj:P * jj + P],
                                              s_sb[:, P * jj:P * jj + P], ident_sb[:, :])
                ins.then_inc(st_done, 1)

            def project_o(b):
                pe.wait_ge(sT_ready, b + 1)
                if b:
                    pe.wait_ge(h2_ready, b)
                for jj in range(4):
                    ins = mm(WO_PS[:, P * jj:P * jj + P], sT_sb[:, P * jj:P * jj + P], wo_bd[:, :],
                             start=jj == 0, stop=jj == 3, skip_group_check=True)
                ins.then_inc(wo_done, 1)

            def transpose_x(b, half):
                pe.wait_ge(xl_ready, b + 1)
                pe.wait_ge(xh_ready, b + 1)
                if b >= 2:
                    pe.wait_ge(xT_ready, 2 * b + half)
                    pe.wait_ge(cwT_ready, 2 * b - 2)
                elif b:
                    pe.wait_ge(xT_ready, half + 1)
                for j in range(4):
                    ins = nc.tensor.transpose(XT_PS[0 if b >= 2 else half][:, P * j:P * j + P],
                                              split_sb[:, 4 * half + j, :, :].rearrange("p k d -> p (k d)"), ident_sb[:, :])
                ins.then_inc(xt_done, 1)

            def gate_logits(b):
                pe.wait_ge(xT_ready, 2 * b + 2)
                if b:
                    pe.wait_ge(z_ready, min(b, 2))
                for g in range(NG):
                    t, o = (NG * b + g) * P, 16 * (NG * (b % 2) + g)
                    ins = mm(LG_PS[:, o:o + 16], xT_all[:, t:t + P], gw_r[:, :],
                             start=g == 0, stop=g == NG - 1, skip_group_check=True)
                ins.then_inc(lg_done, 1)

            def transpose_cw(c):
                pe.wait_ge(cw_ready, c // 2 + 1)
                if c < 4:
                    pe.wait_ge(xT_ready, (4, 4, 6, 6)[c])
                else:
                    pe.wait_ge(y_ready, (3, 3, 3, 4)[c - 4])
                if c:
                    pe.wait_ge(cwT_ready, c)
                g0 = (0, 4, 8, 12, 0, 4, 8, 12)[c]
                for j in range(4):
                    ins = nc.tensor.transpose(CT_PS[c][0:RS * E, P * j:P * j + P],
                                              cw_sp[:, g0 + j, :, :].rearrange("p k e -> p (k e)"), ident_sb[:, :])
                ins.then_inc(ct_done, 1)

            def hidden(c, e, A):
                n = E * c + e
                if is_first(c) and e < 2:
                    if e == 0:
                        pe.wait_ge(hT_ready, B)
                        pe.wait_ge(h_ready, B)
                        pe.wait_ge(w1_ready, 2)
                else:
                    pe.wait_ge(gelu_done, n - (1 if A is A_EARLY else 3))
                if isinstance(c, int) and c == 3 and e == 0:
                    pe.wait_ge(y_ready, 2)
                    pe.wait_ge(xT_ready, NCH)
                xs = xT_all[:, bass.ts(c, CH)]
                mm(A[e % 4][:, :], w1_hi[:, e, :], xs, start=True, stop=False)
                mm(A[e % 4][:, :], w1_lo[:, e, :], xs, start=False, stop=True).then_inc(mm1_done, 1)

            def broadcast(c, k):
                p = PAIRS * c + k
                if is_first(c) and k == 0:
                    pe.wait_ge(g_ready, 3)
                    pe.wait_ge(sel_ready, 1)
                else:
                    pe.wait_ge(cwb_ready, p)
                if k == 0:
                    pe.wait_ge(cwT_ready, c + 1 if isinstance(c, int) else NCH)
                mm(CB_PS[:, :], sel_sb[:, k, :], cwT_all[:, bass.ts(c, CH)], start=True, stop=True).then_inc(cb_done, 1)

            def project_pair(c, k):
                p = PAIRS * c + k
                if is_first(c) and k < 2:
                    if k == 0:
                        pe.wait_ge(w2_ld, 16)
                        pe.wait_ge(sT_ready, 3)
                        pe.wait_ge(xT_ready, 4)
                    else:
                        pe.wait_ge(g_ready, B)
                else:
                    pe.wait_ge(weighted, p - 1)
                pe.wait_ge(gelu_done, 2 * p + 2)
                for i in range(2):
                    e = 2 * k + i
                    ins = mm(Y_PS[k % 2][64 * i:64 * i + 64, :], w2_sb[:, e, :], act_sb[:, e % 4, :], start=True, stop=True)
                ins.then_inc(mm2_done, 1)

            def transpose_out(c, OT_PS):
                pe.wait_ge(added, 3 * c + 3)
                if is_first(c):
                    pe.wait_ge(h2_ready, B)
                else:
                    pe.wait_ge(y_ready, c)
                if isinstance(c, int):
                    if c == 2:
                        pe.wait_ge(z_ready, 3)
                    elif c == 3:
                        pe.wait_ge(cwT_ready, 7)
                for jj in range(4):
                    ins = nc.tensor.transpose(OT_PS[:, P * jj:P * jj + P], fin_sb[:, P * jj:P * jj + P], ident_sb[:, :])
                ins.then_inc(ot_done, 1)

            def moe(c, k, A):
                hidden(c, 2 * k, A)
                hidden(c, 2 * k + 1, A)
                broadcast(c, k)
                if k:
                    project_pair(c, k - 1)
                elif not is_first(c):
                    project_pair(c - 1, PAIRS - 1)

            keep_warm(3)
            pe.wait_ge(weff_ready, 8)
            tokenize(0)
            pe.wait_ge(wgc_ready, 1)
            pe.wait_ge(id_ld, 16)
            h_and_gate(0)
            tokenize(1, range(0, 3))
            transpose_s(0)
            tokenize(1, range(3, 4))
            pe.wait_ge(wo_ready, 1)
            project_o(0)
            for b in (1, 2):
                h_and_gate(b)
                tokenize(b + 1)
                transpose_s(b)
                transpose_x(b - 1, 0)
                transpose_x(b - 1, 1)
                project_o(b)
                if b == 1:
                    pe.wait_ge(gw_ready, 1)
                gate_logits(b - 1)
            h_and_gate(3)
            transpose_cw(0)
            moe(0, 0, A_EARLY)
            transpose_cw(1)
            moe(0, 1, A_EARLY)
            moe(0, 2, A_EARLY)
            transpose_s(3)
            moe(0, 3, A_EARLY)
            moe(1, 0, A_EARLY)
            transpose_x(2, 0)
            project_o(3)
            moe(1, 1, A_EARLY)
            transpose_x(2, 1)
            moe(1, 2, A_EARLY)
            transpose_out(0, OT_EARLY)
            moe(1, 3, A_EARLY)
            transpose_cw(2)
            gate_logits(2)
            moe(2, 0, A_EARLY)
            transpose_cw(3)
            moe(2, 1, A_EARLY)
            transpose_x(3, 0)
            moe(2, 2, A_EARLY)
            transpose_out(1, OT_EARLY)
            transpose_x(3, 1)
            moe(2, 3, A_EARLY)
            gate_logits(3)
            moe(3, 0, A_LATE)
            moe(3, 1, A_LATE)
            moe(3, 2, A_LATE)
            transpose_out(2, OT_LATE)
            moe(3, 3, A_LATE)
            transpose_cw(4)
            moe(4, 0, A_LATE)
            transpose_cw(5)
            moe(4, 1, A_LATE)
            transpose_cw(6)
            moe(4, 2, A_LATE)
            transpose_out(3, OT_LATE)
            moe(4, 3, A_LATE)
            transpose_cw(7)
            with pe.Fori(5, NCH) as c:
                moe(c, 0, A_LATE)
                moe(c, 1, A_LATE)
                moe(c, 2, A_LATE)
                transpose_out(c - 1, OT_LATE)
                moe(c, 3, A_LATE)
            project_pair(NCH - 1, PAIRS - 1)
            transpose_out(NCH - 1, OT_LATE)


_INS = {"x": "x", "W": "L0_tok_W", "wg": "L0_attn_wg", "wo": "L0_attn_wo", "gn_bias": "L0_attn_gn_bias",
        "attn_bias": "L0_attn_bias", "gate_w": "L0_ffn_gate_w", "gate_b": "L0_ffn_gate_b", "W1": "L0_ffn_W1",
        "b1": "L0_ffn_b1", "W2": "L0_ffn_W2", "b2": "L0_ffn_b2"}


def _constants(np):
    f, p = np.arange(NF)[:, None], np.arange(WIN)[None, :]
    angle = 2.0 * np.pi * ((f * p) % WIN) / WIN
    table = np.concatenate([np.cos(angle), -np.sin(angle)]) / np.sqrt(WIN)
    half = np.eye(2)
    return {
        "dft": np.kron(np.eye(DLO), table).astype(np.float32),
        "ident": np.eye(P, dtype=np.float32),
        "center": np.kron(half, np.eye(D) - 1.0 / D).astype(np.float32),
        "rank": (E - np.arange(E, dtype=np.float32))[None, :],
        "sel": np.tile(np.repeat(np.eye(E, dtype=np.float32), D, axis=1).reshape(E, PAIRS, P), (RS, 1, 1)),
    }


def kernel(**inputs):
    import numpy as np
    import concourse.bacc as bacc
    from concourse.bass_utils import run_bass_kernel_spmd

    nc = bacc.Bacc("TRN2", target_bir_lowering=False, num_devices=1)
    data = {k: np.ascontiguousarray(inputs[v]) for k, v in _INS.items()}
    data.update(_constants(np))
    arrays, args = {}, {}
    for name, a in data.items():
        arrays[f"in_{name}"] = a
        args[name] = nc.dram_tensor(f"in_{name}", a.shape, mybir.dt.from_np(a.dtype), kind="ExternalInput").ap()
    out = nc.dram_tensor("out", (B, V * NWIN, D), F32, kind="ExternalOutput").ap()
    vit_layer(nc, out=out, **args)
    r = run_bass_kernel_spmd(nc, [arrays], core_ids=[0])
    return r.results[0]["out"]
```

```python
from contextlib import ExitStack

import concourse.bass as bass
from concourse import mybir

ALU = mybir.AluOpType
ACT = mybir.ActivationFunctionType
F32 = mybir.dt.float32
F32R = mybir.dt.float32r
BF16 = mybir.dt.bfloat16
AX_X = mybir.AxisListType.X

B, C, T, V = 4, 64, 128, 64
WIN, HOP = 16, 8
NF = WIN // 2 + 1
G = 2 * NF
NWIN = T // HOP
D = 64
E, H = 8, 128
EPS = 1e-5
P = 128
DLO = 4
DHI = D // DLO
NG = 8
NCH = 2 * B
CH = 512
PAIRS = E // 2
WARM = 11
RS = 2


def vit_layer(nc, x, W, wg, wo, gn_bias, attn_bias, gate_w, gate_b, W1, b1, W2, b2, dft, ident, center, rank, out):
    ctx = ExitStack()
    with ctx:
        def sb(name, shape, dt=F32):
            return ctx.enter_context(nc.sbuf_tensor(name, shape, dt))

        def sem(name):
            return ctx.enter_context(nc.semaphore(name))

        x_sb = [sb(f"x_{par}", [P, NWIN + 1, 4, V]) for par in range(2)]
        warm = sb("warm", [P, 512], BF16)
        w_rows = sb("w_rows", [DLO * G, DHI, C])
        dft_sb = sb("dft_sb", [DLO * G, 2, DLO * WIN // 2])
        w_eff = sb("w_eff", [P, 2, 4, D])
        ident_sb = sb("ident_sb", [P, P])
        fold_sb = sb("fold_sb", [P, D])
        center_sb = sb("center_sb", [P, P])
        wg_bd = sb("wg_bd", [P, P])
        wgc_bd = sb("wgc_bd", [P, P])
        wo_bd = sb("wo_bd", [P, P])
        gnb = sb("gnb", [P, 1])
        bias_b = sb("bias_b", [P, D])
        gate_b_b = sb("gate_b_b", [P, E])
        rank_b = sb("rank_b", [P, E])
        gw_raw = sb("gw_raw", [P, E])
        gw_r = sb("gw_r", [P, RS * E], F32R)
        w1_raw = sb("w1_raw", [P, E, H])
        w1_hi = sb("w1_hi", [P, E, H], F32R)
        w1_lo = sb("w1_lo", [P, E, H], F32R)
        w2_sb = sb("w2_sb", [P, E, D])
        b1_sb = sb("b1_sb", [P, E])
        b2_sb = sb("b2_sb", [P, PAIRS])
        expo = sb("expo", [P, NG])

        hT_sb = sb("hT_sb", [P, CH])
        h_sb = sb("h_sb", [P, NG, D])
        hb_sb = sb("hb_sb", [P, NG, D])
        g_sb = sb("g_sb", [P, NG * D])
        th_sb = sb("th_sb", [P, NG * D])
        s_sb = sb("s_sb", [P, NG * D])
        sT_sb = sb("sT_sb", [P, CH])
        st1 = sb("st1", [P, NG, 6])
        st2 = sb("st2", [P, NG, 6])
        sm1 = sb("sm1", [P, 6, NG])
        sm2 = sb("sm2", [P, 6, NG])
        h2_all = sb("h2_all", [P, NCH * 4, D])
        xc_sb = sb("xc_sb", [P, NG, D])
        xn_sb = sb("xn_sb", [P, NG, D])
        split_sb = sb("split_sb", [P, NG, RS, D])
        xT_all = sb("xT_all", [P, NCH * CH], F32R)
        lz = sb("lz", [P, 6, 2 * NG, E])
        lm = sb("lm", [P, 7, 2 * NG])
        table_sb = sb("table_sb", [P, 1])
        cw = sb("cw", [P, 2 * NG, E])
        cwT_all = sb("cwT_all", [E, NCH * CH])
        act_sb = sb("act_sb", [P, 4, CH])
        cwb_sb = sb("cwb_sb", [P, PAIRS, CH])
        yw_sb = sb("yw_sb", [P, PAIRS, CH])
        acc_sb = sb("acc_sb", [P, CH])
        fin_sb = sb("fin_sb", [P, CH])
        y_sb = sb("y_sb", [P, 4, D])
        o_sb = sb("o_sb", [P, 4, D])

        bank = [ctx.enter_context(nc.psum_tensor(f"bank{i}", [P, 512], F32)) for i in range(8)]
        HP_PS, GP_PS, ST_PS, WO_PS, LG_PS = (bank[i] for i in (1, 2, 3, 4, 7))
        XT_PS = [bank[5], bank[6]]
        W_EFF_PS = [HP_PS, GP_PS]
        HT_PS = [bank[0], bank[6], bank[0], bank[0]]
        GATE_PS = [GP_PS] * 3 + [bank[6]]
        A_EARLY, A_LATE = [bank[0], bank[1], bank[0], bank[1]], [bank[4], bank[5], bank[0], bank[1]]
        LAST_Y_PS, FOLD_PS = [bank[6], bank[5]], [bank[7], bank[4]]
        CT_PS, Y_PS, OT_EARLY, OT_LATE = bank[2], [bank[3], bank[6]], bank[4], bank[7]

        x_first = [sem(f"x_first_{b}") for b in range(2)]
        x_ld = [sem(f"x_ld_{par}") for par in range(2)]
        w_ld, id_ld, wg_ld, wo_ld, bias_ld, vec_ld, w1_ld, w2_ld = (
            sem(n) for n in "w_ld id_ld wg_ld wo_ld bias_ld vec_ld w1_ld w2_ld".split())
        warm_set, zeroed = sem("warm_set"), sem("zeroed")
        weff_mm, weff_ready, wgc_mm, wgc_ready = (sem(n) for n in "weff_mm weff_ready wgc_mm wgc_ready".split())
        wo_ready, gw_ready, w1_ready = (sem(n) for n in "wo_ready gw_ready w1_ready".split())
        tok_done, hT_ready, hp_done, hg_done, h_ready, var1, rstd1, g_ready, tanh_done = (
            sem(n) for n in "tok_done hT_ready hp_done hg_done h_ready var1 rstd1 g_ready tanh_done".split())
        s_ready, st_done, sT_ready, wo_done, hb_ready, h2_ready, var2, rstd2, xn_ready, xh_ready, xl_ready = (
            sem(n) for n in "s_ready st_done sT_ready wo_done hb_ready h2_ready var2 rstd2 xn_ready xh_ready xl_ready".split())
        xt_done, xT_ready, lg_done, z_ready, exp_done, cw_ready, ct_done, cwT_ready = (
            sem(n) for n in "xt_done xT_ready lg_done z_ready exp_done cw_ready ct_done cwT_ready".split())
        cwb_ld = [sem(f"cwb_ld_{k}") for k in range(PAIRS)]
        mm1_done, gelu_done, mm2_done, weighted, added, ot_done, y1_done, y_ready, out_st = (
            sem(n) for n in "mm1_done gelu_done mm2_done weighted added ot_done y1_done y_ready out_st".split())
        fold_ready, last_mm2, last_weighted, last_added, folded = (
            sem(n) for n in "fold_ready last_mm2 last_weighted last_added folded".split())
        dve_step = sem("dve_step")

        def grp(ap):
            return ap.rearrange("p (j h d) -> p j h d", j=4, h=2)

        def is_first(c):
            return isinstance(c, int) and c == 0

        def move_w_eff(copy, n):
            for hop in range(2):
                src = W_EFF_PS[n][:, 0:256].rearrange("c (h l k s) -> c k s h l", h=8, l=DLO, k=2)[:, hop, :, :, :]
                dst = w_eff[:, hop, :, :].rearrange("c s (m h l) -> c m s h l", l=DLO, m=2)[:, n, :, :, :]
                copy(dst, src).then_inc(weff_ready, 1)

        block = ctx.enter_context(nc.Block())

        @block.sync
        def _(sp):
            xv = x.rearrange("b c (m h s) v -> b h c m s v", h=2, s=4)

            def load_edge(b, done):
                for half in range(2):
                    sp.dma_start(x_sb[b % 2][64 * half:64 * half + 64, NWIN, :, :],
                                 x[b, :, T - 1:T, :].to_broadcast([C, 4, V])).then_inc(done, 16)

            def load_x(b, steps, done):
                for half in range(2):
                    sp.dma_start(x_sb[b % 2][64 * half:64 * half + 64, 0:NWIN, steps, :], xv[b, half, :, :, steps, :]
                                 ).then_inc(done, 16)

            wv = W.rearrange("(h l) (g c) -> (l g) h c", l=DLO, c=C)
            for n in range(2):
                sp.dma_start(w_rows[:, 8 * n:8 * n + 8, :], wv[:, 8 * n:8 * n + 8, :]).then_inc(w_ld, 16)
            for b in range(2):
                load_x(b, slice(0, 2), x_first[b])
                load_edge(b, x_first[b])
                load_x(b, slice(2, 4), x_ld[b])
            sp.wait_ge(zeroed, 2)
            for hi in range(2):
                sp.dma_start(wo_bd[64 * hi:64 * hi + 64, 64 * hi:64 * hi + 64], wo).then_inc(wo_ld, 16)
                sp.dma_start(gnb[64 * hi:64 * hi + 64, :], gn_bias.rearrange("(d o) -> d o", o=1)).then_inc(wo_ld, 16)
            sp.dma_start(bias_b[:, :], attn_bias.rearrange("(o d) -> o d", o=1).to_broadcast([P, D])).then_inc(bias_ld, 16)
            for hi in range(2):
                sp.dma_start(w1_raw[64 * hi:64 * hi + 64, :, :], W1.rearrange("e d h -> d e h")).then_inc(w1_ld, 16)
            for b in (2, 3):
                sp.wait_ge(tok_done, b - 1)
                load_x(b, slice(0, 4), x_ld[b % 2])
                load_edge(b, x_ld[b % 2])
                if b == 2:
                    sp.dma_start(gate_b_b[:, :], gate_b.rearrange("(o e) -> o e", o=1).to_broadcast([P, E])).then_inc(vec_ld, 16)
                    sp.dma_start(rank_b[:, :], rank.to_broadcast([P, E])).then_inc(vec_ld, 16)
                    sp.dma_start(b1_sb[:, :], b1.rearrange("e h -> h e"), allow_slow_non_contiguous=True).then_inc(vec_ld, 16)
                    b2v = b2.rearrange("(k i) d -> i d k", i=2)
                    for i in range(2):
                        sp.dma_start(gw_raw[64 * i:64 * i + 64, :], gate_w).then_inc(vec_ld, 16)
                        sp.dma_start(b2_sb[64 * i:64 * i + 64, :], b2v[i], allow_slow_non_contiguous=True).then_inc(vec_ld, 16)
                    sp.dma_start(w2_sb[:, :, :], W2.rearrange("e h d -> h e d")).then_inc(w2_ld, 16)
            ov = out.rearrange("b (v h k j) d -> b h k v j d", h=2, k=2, j=4)

            def load_cwb(c, k):
                if k == 0:
                    sp.wait_ge(cwT_ready, c + 1)
                if c:
                    sp.wait_ge(weighted, PAIRS * (c - 1) + k + 1)
                for i in range(2):
                    e = 2 * k + i
                    sp.dma_start(cwb_sb[64 * i:64 * i + 64, k, :],
                                 cwT_all[e:e + 1, None, c * CH:(c + 1) * CH].to_broadcast([1, D, CH])
                                 ).then_inc(cwb_ld[k], 16)

            def store(b, hi, ready):
                sp.wait_ge(y_ready, ready)
                for j4 in range(2):
                    sp.dma_start(ov[b, hi, j4, :, :, :], o_sb[64 * j4:64 * j4 + 64, :, :]).then_inc(out_st, 16)

            for c in range(NCH):
                for k in range(PAIRS):
                    load_cwb(c, k)
                    if k == 1 and c > 1:
                        store((c - 2) // 2, (c - 2) % 2, c - 1)
            store(B - 1, 0, NCH - 1)
            store(B - 1, 1, NCH + 1)
            sp.wait_ge(out_st, 32 * NCH)

        @block.gpsimd
        def _(pool):
            for t in (wg_bd, wo_bd):
                nc.gpsimd.memset(t[:, :], 0.0).then_inc(zeroed, 1)
            nc.gpsimd.memset(expo[:, :], -0.5).then_inc(zeroed, 1)
            pool.wait_ge(zeroed, 3)
            pool.wait_ge(id_ld, 16)
            nc.gpsimd.tensor_tensor(fold_sb[:, :], ident_sb[:, 0:D], ident_sb[:, D:P], ALU.add).then_inc(fold_ready, 1)
            pool.wait_ge(bias_ld, 16)

            def add_bias(b):
                pool.wait_ge(h_ready, b + 1)
                if b:
                    pool.wait_ge(h2_ready, b)
                nc.gpsimd.tensor_tensor(hb_sb[:, :, :], h_sb[:, :, :], bias_b[:, None, :].to_broadcast([P, NG, D]),
                                        ALU.add).then_inc(hb_ready, 1)

            def rsqrt(sm, ready, done, b):
                pool.wait_ge(ready, b + 1)
                nc.gpsimd.tensor_tensor(sm[:, 5, :], sm[:, 4, :], expo[:, :], ALU.pow).then_inc(done, 1)

            def low_part(b):
                pool.wait_ge(xn_ready, b + 1)
                pool.wait_ge(xh_ready, b + 1)
                nc.gpsimd.tensor_tensor(split_sb[:, :, 1, :], xn_sb[:, :, :], split_sb[:, :, 0, :], ALU.subtract
                                        ).then_inc(xl_ready, 1)

            def accumulate(c, k):
                pool.wait_ge(weighted, PAIRS * c + k + 1)
                dst = acc_sb if k < PAIRS - 1 else fin_sb
                if not (is_first(c) and k == 1):
                    pool.wait_ge(added, 3 * c + k - 1)
                if k == PAIRS - 1 and not is_first(c):
                    pool.wait_ge(ot_done, c)
                so_far = yw_sb[:, 0, :] if k == 1 else acc_sb[:, :]
                nc.gpsimd.tensor_tensor(dst[:, :], yw_sb[:, k, :], so_far, ALU.add).then_inc(added, 1)

            for b in range(3):
                if b:
                    rsqrt(sm2, var2, rstd2, b - 1)
                rsqrt(sm1, var1, rstd1, b)
                if b:
                    low_part(b - 1)
                add_bias(b)
            rsqrt(sm1, var1, rstd1, 3)
            rsqrt(sm2, var2, rstd2, 2)
            add_bias(3)
            low_part(2)
            accumulate(0, 1)
            accumulate(0, 2)
            accumulate(0, 3)
            rsqrt(sm2, var2, rstd2, 3)
            accumulate(1, 1)
            low_part(3)
            accumulate(1, 2)
            accumulate(1, 3)
            for c in range(2, 4):
                for k in range(1, PAIRS):
                    accumulate(c, k)
            accumulate(4, 1)
            with pool.Fori(5, NCH) as c:
                accumulate(c - 1, 2)
                accumulate(c - 1, 3)
                accumulate(c, 1)

        @block.scalar
        def _(act):
            act.dma_start(dft_sb[:, :, :].rearrange("k h n -> k (h n)"), dft).then_inc(w_ld, 16)
            act.dma_start(center_sb[:, :], center).then_inc(wg_ld, 16)
            act.wait_ge(zeroed, 3)
            for hi in range(2):
                act.dma_start(wg_bd[64 * hi:64 * hi + 64, 64 * hi:64 * hi + 64], wg).then_inc(wg_ld, 16)
            act.dma_start(ident_sb[:, :], ident).then_inc(id_ld, 16)

            act.wait_ge(weff_mm, 2)
            move_w_eff(nc.scalar.copy, 1)

            def evac_hT(b):
                act.wait_ge(tok_done, b + 1)
                if b:
                    act.wait_ge(hg_done, b)
                nc.scalar.activation(hT_sb[:, :], HT_PS[b][:, :], ACT.Copy).then_inc(hT_ready, 1)

            def evac_h(b):
                act.wait_ge(hp_done, b + 1)
                if b:
                    act.wait_ge(var1, b)
                    act.wait_ge(hb_ready, b)
                nc.scalar.activation(h_sb[:, :, :].rearrange("p g d -> p (g d)"), HP_PS[:, :], ACT.Copy).then_inc(h_ready, 1)

            def tanh(b):
                act.wait_ge(g_ready, b + 1)
                if b:
                    act.wait_ge(s_ready, b)
                nc.scalar.activation(th_sb[:, :], g_sb[:, :], ACT.Tanh, scale=0.5).then_inc(tanh_done, 1)

            def evac_sT(b):
                act.wait_ge(st_done, b + 1)
                if b:
                    act.wait_ge(wo_done, b)
                nc.scalar.activation(sT_sb[:, :], (WO_PS if b == 3 else ST_PS)[:, :], ACT.Copy).then_inc(sT_ready, 1)

            def high_part(b):
                act.wait_ge(xn_ready, b + 1)
                if b:
                    act.wait_ge(xt_done, 2 * b)
                nc.scalar.activation(split_sb[:, :, 0, :].bitcast(F32R), xn_sb[:, :, :], ACT.Copy).then_inc(xh_ready, 1)

            def evac_xT(b, half):
                act.wait_ge(xt_done, 2 * b + half + 1)
                c = 2 * b + half
                nc.scalar.activation(xT_all[:, c * CH:(c + 1) * CH], XT_PS[0 if b >= 2 else half][:, :], ACT.Copy
                                     ).then_inc(xT_ready, 1)

            def exp(g0, n, count):
                act.wait_ge(z_ready, count)
                nc.scalar.activation(lz[:, 2, g0:g0 + n, :], lz[:, 1, g0:g0 + n, :], ACT.Exp).then_inc(exp_done, 1)

            def evac_cwT(c):
                act.wait_ge(ct_done, c + 1)
                nc.scalar.activation(cwT_all[:, c * CH:(c + 1) * CH], CT_PS[0:E, :], ACT.Copy
                                     ).then_inc(cwT_ready, 1)

            def moe(c, k, A):
                p = PAIRS * c + k
                for i in range(2):
                    e = 2 * k + i
                    act.wait_ge(mm1_done, E * c + e + 1)
                    if i == 0 and not (is_first(c) and k < 2):
                        act.wait_ge(mm2_done, p - 1)
                    nc.scalar.activation(act_sb[:, e % 4, :], A[e % 4][:, :], ACT.Gelu, bias=b1_sb[:, e:e + 1]
                                         ).then_inc(gelu_done, 1)

            evac_hT(0)
            evac_h(0)
            tanh(0)
            evac_sT(0)
            evac_hT(1)
            evac_h(1)
            high_part(0)
            tanh(1)
            evac_hT(2)
            evac_sT(1)
            evac_xT(0, 0)
            evac_h(2)
            evac_xT(0, 1)
            high_part(1)
            exp(0, NG, 1)
            tanh(2)
            evac_hT(3)
            evac_xT(1, 0)
            evac_xT(1, 1)
            evac_sT(2)
            evac_h(3)
            exp(NG, NG, 2)
            act.wait_ge(vec_ld, 16 * 7)
            nc.scalar.activation(table_sb[:, :], b1_sb[:, 0:1], ACT.Gelu)
            moe(0, 0, A_EARLY)
            evac_cwT(0)
            moe(0, 1, A_EARLY)
            evac_cwT(1)
            tanh(3)
            moe(0, 2, A_EARLY)
            moe(0, 3, A_EARLY)
            evac_sT(3)
            moe(1, 0, A_EARLY)
            high_part(2)
            moe(1, 1, A_EARLY)
            evac_xT(2, 0)
            moe(1, 2, A_EARLY)
            evac_xT(2, 1)
            moe(1, 3, A_EARLY)
            evac_cwT(2)
            moe(2, 0, A_EARLY)
            high_part(3)
            moe(2, 1, A_EARLY)
            evac_cwT(3)
            evac_xT(3, 0)
            moe(2, 2, A_EARLY)
            evac_xT(3, 1)
            moe(2, 3, A_EARLY)
            moe(3, 0, A_LATE)
            exp(0, 2 * NG, 3)
            moe(3, 1, A_LATE)
            moe(3, 2, A_LATE)
            evac_cwT(4)
            moe(3, 3, A_LATE)
            evac_cwT(5)
            moe(4, 0, A_LATE)
            moe(4, 1, A_LATE)
            evac_cwT(6)
            moe(4, 2, A_LATE)
            moe(4, 3, A_LATE)
            evac_cwT(7)
            with act.Fori(5, NCH) as c:
                for k in range(PAIRS):
                    moe(c, k, A_LATE)

        @block.vector
        def _(dve):
            steps = [0]

            def link(ins):
                steps[0] += 1
                ins.then_inc(dve_step, 1)
                dve.wait_ge(dve_step, steps[0])

            nc.vector.memset(warm[:, :], 0.0).then_inc(warm_set, 1)
            dve.wait_ge(weff_mm, 1)
            move_w_eff(nc.vector.tensor_copy, 0)
            dve.wait_ge(wgc_mm, 1)
            nc.vector.tensor_copy(wgc_bd[:, :], ST_PS[:, 0:P]).then_inc(wgc_ready, 1)
            dve.wait_ge(wo_ld, 16 * 4)
            nc.vector.tensor_scalar(wo_bd[:, :], wo_bd[:, :], gnb[:, 0:1], 0.5, ALU.mult, ALU.mult).then_inc(wo_ready, 1)

            def prep_gate():
                dve.wait_ge(vec_ld, 16 * 7)
                link(nc.vector.tensor_copy(gw_r[:, 0:E], gw_raw[:, :]))
                nc.vector.tensor_tensor(gw_r[:, E:2 * E], gw_raw[:, :], gw_r[:, 0:E].bitcast(F32), ALU.subtract
                                        ).then_inc(gw_ready, 1)

            def prep_w1(part):
                es = slice(4 * part, 4 * part + 4)
                dve.wait_ge(w1_ld, 32)
                link(nc.vector.tensor_copy(w1_hi[:, es, :], w1_raw[:, es, :]))
                nc.vector.tensor_tensor(w1_lo[:, es, :], w1_raw[:, es, :], w1_hi[:, es, :].bitcast(F32), ALU.subtract
                                        ).then_inc(w1_ready, 1)

            def moments(src, st):
                for g in range(NG):
                    nc.vector.bn_stats(st[:, g, :], src[:, g, :]).then_inc(dve_step, 1)
                steps[0] += NG

            def combine(st, sm, done, mean):
                dve.wait_ge(dve_step, steps[0])
                me, m2e, mo, m2o = (st[:, :, k] for k in (1, 2, 4, 5))
                nc.vector.tensor_tensor(sm[:, 1, :], m2e, m2o, ALU.add).then_inc(dve_step, 1)
                if mean:
                    nc.vector.tensor_tensor(sm[:, 2, :], me, mo, ALU.add).then_inc(dve_step, 1)
                nc.vector.tensor_tensor(sm[:, 0, :], me, mo, ALU.subtract).then_inc(dve_step, 1)
                steps[0] += 3 if mean else 2
                dve.wait_ge(dve_step, steps[0])
                link(nc.vector.tensor_tensor(sm[:, 3, :], sm[:, 0, :], sm[:, 0, :], ALU.mult))
                link(nc.vector.scalar_tensor_tensor(sm[:, 0, :], sm[:, 3, :], D / 4.0, sm[:, 1, :], ALU.mult, ALU.add))
                nc.vector.tensor_scalar(sm[:, 4, :], sm[:, 0, :], 1.0 / D, EPS, ALU.mult, ALU.add).then_inc(done, 1)
                if mean:
                    nc.vector.tensor_scalar(sm[:, 3, :], sm[:, 2, :], 0.5, None, ALU.mult).then_inc(dve_step, 1)
                    steps[0] += 1

            def ln1_stats(b):
                dve.wait_ge(h_ready, b + 1)
                moments(h_sb, st1)
                combine(st1, sm1, var1, False)

            def scale_g(b):
                dve.wait_ge(rstd1, b + 1)
                dve.wait_ge(hg_done, b + 1)
                nc.vector.tensor_tensor(g_sb[:, :].rearrange("p (g d) -> p g d", g=NG),
                                        GATE_PS[b][:, :].rearrange("p (g d) -> p g d", g=NG),
                                        sm1[:, 5, :, None].to_broadcast([P, NG, D]), ALU.mult).then_inc(g_ready, 1)

            def silu(b):
                dve.wait_ge(tanh_done, b + 1)
                if b:
                    dve.wait_ge(st_done, b)
                nc.vector.scalar_tensor_tensor(s_sb[:, :], th_sb[:, :], 1.0, g_sb[:, :], ALU.add, ALU.mult
                                               ).then_inc(s_ready, 1)

            def residual(b):
                dve.wait_ge(wo_done, b + 1)
                dve.wait_ge(hb_ready, b + 1)
                nc.vector.tensor_tensor(h2_all[:, 8 * b:8 * b + 8, :].rearrange("p (h j) d -> p j h d", h=2),
                                        grp(WO_PS[:, :]), grp(hb_sb[:, :, :].rearrange("p g d -> p (g d)")),
                                        ALU.add).then_inc(h2_ready, 1)

            def ln2_moments(b):
                dve.wait_ge(h2_ready, b + 1)
                moments(h2_all[:, 8 * b:8 * b + 8, :], st2)

            def ln2_combine():
                combine(st2, sm2, var2, True)

            def ln2_center(b):
                dve.wait_ge(dve_step, steps[0])
                link(nc.vector.tensor_tensor(xc_sb[:, :, :], h2_all[:, 8 * b:8 * b + 8, :],
                                             sm2[:, 3, :, None].to_broadcast([P, NG, D]), ALU.subtract))

            def ln2_scale(b):
                dve.wait_ge(rstd2, b + 1)
                if b:
                    dve.wait_ge(xh_ready, b)
                    dve.wait_ge(xl_ready, b)
                nc.vector.tensor_tensor(xn_sb[:, :, :], xc_sb[:, :, :], sm2[:, 5, :, None].to_broadcast([P, NG, D]),
                                        ALU.mult).then_inc(xn_ready, 1)

            def logits(g0, n, count):
                dve.wait_ge(lg_done, count)
                lg = LG_PS[:, 16 * g0:16 * (g0 + n)].rearrange("p (g k e) -> p g k e", g=n, k=2)
                gs, bc = slice(g0, g0 + n), [P, n, E]
                link(nc.vector.tensor_tensor(lz[:, 0, gs, :], lg[:, :, 0, :], gate_b_b[:, None, :].to_broadcast(bc), ALU.add))
                link(nc.vector.tensor_tensor(lz[:, 3, gs, :], lg[:, :, 1, :], lz[:, 0, gs, :], ALU.add))
                link(nc.vector.tensor_reduce(lm[:, 0, gs], lz[:, 3, gs, :], AX_X, ALU.max))
                nc.vector.tensor_tensor(lz[:, 1, gs, :], lz[:, 3, gs, :], lm[:, 0, gs, None].to_broadcast(bc),
                                        ALU.subtract).then_inc(z_ready, 1)

            def route_top(g0, n, count):
                gs, bc = slice(g0, g0 + n), [P, n, E]
                z, key, hot1 = (lz[:, k, gs, :] for k in (1, 3, 4))
                dve.wait_ge(z_ready, count)
                link(nc.vector.scalar_tensor_tensor(key, z, 0.0, rank_b[:, None, :].to_broadcast(bc), ALU.is_equal, ALU.mult))
                link(nc.vector.tensor_reduce(lm[:, 3, gs], key, AX_X, ALU.max))
                link(nc.vector.tensor_tensor(hot1, key, lm[:, 3, gs, None].to_broadcast(bc), ALU.is_equal))

            def route_sum(g0, n, count):
                gs = slice(g0, g0 + n)
                dve.wait_ge(exp_done, count)
                link(nc.vector.tensor_reduce(lm[:, 1, gs], lz[:, 2, gs, :], AX_X, ALU.add))
                link(nc.vector.reciprocal(lm[:, 2, gs], lm[:, 1, gs]))

            def route_second(g0, n):
                gs, bc = slice(g0, g0 + n), [P, n, E]
                ex, key, hot1, rest = (lz[:, k, gs, :] for k in (2, 3, 4, 5))
                link(nc.vector.scalar_tensor_tensor(rest, hot1, -2.0, ex, ALU.mult, ALU.add))
                link(nc.vector.tensor_reduce(lm[:, 4, gs], rest, AX_X, ALU.max))
                link(nc.vector.tensor_tensor(key, rest, lm[:, 4, gs, None].to_broadcast(bc), ALU.is_equal))
                link(nc.vector.tensor_tensor(key, key, rank_b[:, None, :].to_broadcast(bc), ALU.mult))
                link(nc.vector.tensor_reduce(lm[:, 5, gs], key, AX_X, ALU.max))
                link(nc.vector.tensor_tensor(rest, key, lm[:, 5, gs, None].to_broadcast(bc), ALU.is_equal))

            def route_weights(g0, n, ct):
                gs, bc = slice(g0, g0 + n), [P, n, E]
                ex, key, hot1, hot2 = (lz[:, k, gs, :] for k in (2, 3, 4, 5))
                link(nc.vector.tensor_tensor(key, hot1, hot2, ALU.add))
                link(nc.vector.tensor_tensor(key, ex, key, ALU.mult))
                if ct:
                    dve.wait_ge(ct_done, ct)
                nc.vector.tensor_tensor(cw[:, gs, :], key, lm[:, 2, gs, None].to_broadcast(bc), ALU.mult
                                        ).then_inc(cw_ready, 1)

            def weigh(c, k):
                p = PAIRS * c + k
                dve.wait_ge(mm2_done, p + 1)
                dve.wait_ge(cwb_ld[k], 32 * (c + 1))
                if not is_first(c):
                    dve.wait_ge(added, 3 * (c - 1) + max(k, 1))
                nc.vector.scalar_tensor_tensor(yw_sb[:, k, :], Y_PS[k % 2][:, :],
                                               b2_sb[:, k:k + 1], cwb_sb[:, k, :], ALU.add, ALU.mult
                                               ).then_inc(weighted, 1)

            def finish(c, OT_PS):
                dve.wait_ge(ot_done, c + 1)
                ot = OT_PS[:, :].rearrange("p (j k d) -> p j k d", j=4, k=2)
                nc.vector.tensor_tensor(y_sb[:, :, :], ot[:, :, 0, :], h2_all[:, bass.ts(c, 4), :], ALU.add
                                        ).then_inc(y1_done, 1)
                dve.wait_ge(y1_done, c + 1)
                if not is_first(c):
                    dve.wait_ge(out_st, 32 * c)
                nc.vector.tensor_tensor(o_sb[:, :, :], ot[:, :, 1, :], y_sb[:, :, :], ALU.add).then_inc(y_ready, 1)

            for b in range(3):
                if b:
                    residual(b - 1)
                    ln2_moments(b - 1)
                    ln2_combine()
                ln1_stats(b)
                if b:
                    ln2_center(b - 1)
                    ln2_scale(b - 1)
                if b == 2:
                    logits(0, NG, 1)
                scale_g(b)
                if b == 2:
                    route_top(0, NG, 1)
                silu(b)
                if b < 2:
                    prep_w1(b)
                if b == 1:
                    prep_gate()
            route_sum(0, NG, 1)
            route_second(0, NG)
            logits(NG, NG, 2)
            route_weights(0, NG, 0)
            ln1_stats(3)
            residual(2)
            ln2_moments(2)
            scale_g(3)
            silu(3)
            weigh(0, 0)
            ln2_combine()
            ln2_center(2)
            weigh(0, 1)
            ln2_scale(2)
            weigh(0, 2)
            route_top(NG, NG, 2)
            route_sum(NG, NG, 2)
            weigh(0, 3)
            route_second(NG, NG)
            residual(3)
            weigh(1, 0)
            ln2_moments(3)
            ln2_combine()
            route_weights(NG, NG, 2)
            weigh(1, 1)
            ln2_center(3)
            ln2_scale(3)
            weigh(1, 2)
            finish(0, OT_EARLY)
            weigh(1, 3)
            weigh(2, 0)
            weigh(2, 1)
            finish(1, OT_EARLY)
            weigh(2, 2)
            logits(0, 2 * NG, 4)
            weigh(2, 3)
            route_top(0, NG, 3)
            route_sum(0, NG, 3)
            weigh(3, 0)
            route_second(0, NG)
            route_weights(0, NG, 4)
            finish(2, OT_LATE)
            weigh(3, 1)
            route_top(NG, NG, 3)
            route_sum(NG, NG, 3)
            weigh(3, 2)
            route_second(NG, NG)
            weigh(3, 3)
            route_weights(NG, NG, 4)
            weigh(4, 0)
            weigh(4, 1)
            finish(3, OT_LATE)
            weigh(4, 2)
            with dve.Fori(5, NCH) as c:
                weigh(c - 1, 3)
                weigh(c, 0)
                weigh(c, 1)
                finish(c - 1, OT_LATE)
                weigh(c, 2)
            dve.wait_ge(added, 3 * (NCH - 1) + 1)
            dve.wait_ge(cwb_ld[PAIRS - 1], 32 * NCH)
            for half in range(2):
                cols = slice(256 * half, 256 * half + 256)
                dve.wait_ge(last_mm2, half + 1)
                nc.vector.scalar_tensor_tensor(yw_sb[:, PAIRS - 1, cols], LAST_Y_PS[half][:, cols], b2_sb[:, PAIRS - 1:PAIRS],
                                               cwb_sb[:, PAIRS - 1, cols], ALU.add, ALU.mult).then_inc(last_weighted, 1)
            dve.wait_ge(weighted, PAIRS * NCH - 1)
            dve.wait_ge(ot_done, NCH - 1)
            nc.vector.tensor_tensor(fin_sb[:, :], yw_sb[:, PAIRS - 2, :], acc_sb[:, :], ALU.add).then_inc(last_added, 1)
            dve.wait_ge(out_st, 32 * (NCH - 1))
            for half in range(2):
                js = slice(2 * half, 2 * half + 2)
                dve.wait_ge(folded, half + 1)
                nc.vector.tensor_tensor(o_sb[:, js, :], FOLD_PS[half][:, 0:2 * D].rearrange("p (j d) -> p j d", j=2),
                                        h2_all[:, 4 * (NCH - 1) + 2 * half:4 * (NCH - 1) + 2 * half + 2, :], ALU.add
                                        ).then_inc(y_ready, 1)

        @block.tensor
        def _(pe):
            mm = nc.tensor.matmul

            def keep_warm(n):
                for _ in range(n):
                    mm(bank[7][:, :], warm[:, 0:P], warm[:, :], start=True, stop=True, skip_group_check=True)

            pe.wait_ge(warm_set, 1)
            keep_warm(WARM)

            pe.wait_ge(w_ld, 16 * 3)
            for h in range(DHI):
                for half in range(2):
                    ins = mm(W_EFF_PS[h // 8][64 * half:64 * half + 64, 32 * (h % 8):32 * (h % 8) + 32],
                             w_rows[:, h, :], dft_sb[:, half, :], start=h % 8 == 0, stop=h % 8 == 7, skip_group_check=True)
                if h % 8 == 7:
                    ins.then_inc(weff_mm, 1)
            pe.wait_ge(wg_ld, 16 * 3)
            mm(ST_PS[:, 0:P], center_sb[:, :], wg_bd[:, :], start=True, stop=True).then_inc(wgc_mm, 1)

            def tokenize(b, parts=range(8)):
                if b < 2:
                    pe.wait_ge(x_first[b], 16 * 4)
                elif parts[0] == 0:
                    pe.wait_ge(x_ld[b % 2], 32 + 64)
                    pe.wait_ge(hT_ready, b)
                for part in parts:
                    s, hop = part // 2, part % 2
                    if b < 2 and part == 4:
                        pe.wait_ge(x_ld[b], 32)
                    for hi in range(2):
                        blk = 8 * hi + hop
                        win = x_sb[b % 2][:, blk:blk + 8, s, :].rearrange("k (a j) v -> k j a v", a=2)
                        ins = mm(HT_PS[b][64 * hi:64 * hi + 64, :], w_eff[:, hop, s, :], win,
                                 start=part == 0, stop=part == 7)
                if parts[-1] == 7:
                    ins.then_inc(tok_done, 1)

            def transpose_h(b):
                pe.wait_ge(hT_ready, b + 1)
                if b:
                    pe.wait_ge(h_ready, b)
                for jj in range(4):
                    ins = nc.tensor.transpose(HP_PS[:, P * jj:P * jj + P], hT_sb[:, P * jj:P * jj + P], ident_sb[:, :])
                ins.then_inc(hp_done, 1)

            def project_g(b):
                if b:
                    pe.wait_ge(g_ready, b)
                if b == 3:
                    pe.wait_ge(xT_ready, 4)
                for jj in range(4):
                    ins = mm(GATE_PS[b][:, P * jj:P * jj + P], hT_sb[:, P * jj:P * jj + P], wgc_bd[:, :],
                             start=jj == 0, stop=jj == 3, skip_group_check=True)
                ins.then_inc(hg_done, 1)

            def transpose_s(b):
                pe.wait_ge(s_ready, b + 1)
                if b:
                    pe.wait_ge(sT_ready, b)
                if b == 3:
                    pe.wait_ge(h2_ready, 3)
                for jj in range(4):
                    ins = nc.tensor.transpose((WO_PS if b == 3 else ST_PS)[:, P * jj:P * jj + P],
                                              s_sb[:, P * jj:P * jj + P], ident_sb[:, :])
                ins.then_inc(st_done, 1)

            def project_o(b):
                pe.wait_ge(sT_ready, b + 1)
                if b:
                    pe.wait_ge(h2_ready, b)
                for jj in range(4):
                    ins = mm(WO_PS[:, P * jj:P * jj + P], sT_sb[:, P * jj:P * jj + P], wo_bd[:, :],
                             start=jj == 0, stop=jj == 3, skip_group_check=True)
                ins.then_inc(wo_done, 1)

            def transpose_x(b, half):
                pe.wait_ge(xl_ready, b + 1)
                pe.wait_ge(xh_ready, b + 1)
                if b >= 2:
                    pe.wait_ge(xT_ready, 2 * b + half)
                elif b:
                    pe.wait_ge(xT_ready, half + 1)
                for j in range(4):
                    ins = nc.tensor.transpose(XT_PS[0 if b >= 2 else half][:, P * j:P * j + P],
                                              split_sb[:, 4 * half + j, :, :].rearrange("p k d -> p (k d)"), ident_sb[:, :])
                ins.then_inc(xt_done, 1)

            def gate_logits(b):
                pe.wait_ge(xT_ready, 2 * b + 2)
                if b:
                    pe.wait_ge(z_ready, min(b, 2))
                for g in range(NG):
                    t, o = (NG * b + g) * P, 16 * (NG * (b % 2) + g)
                    ins = mm(LG_PS[:, o:o + 16], xT_all[:, t:t + P], gw_r[:, :],
                             start=g == 0, stop=g == NG - 1, skip_group_check=True)
                ins.then_inc(lg_done, 1)

            def transpose_cw(c):
                pe.wait_ge(cw_ready, c // 2 + 1)
                if c:
                    pe.wait_ge(cwT_ready, c)
                else:
                    pe.wait_ge(g_ready, 3)
                g0 = 4 * (c % 4)
                for j in range(4):
                    ins = nc.tensor.transpose(CT_PS[0:E, P * j:P * j + P], cw[:, g0 + j, :], ident_sb[:, :])
                ins.then_inc(ct_done, 1)

            def hidden(c, e, A):
                n = E * c + e
                if is_first(c) and e < 2:
                    if e == 0:
                        pe.wait_ge(hT_ready, B)
                        pe.wait_ge(h_ready, B)
                        pe.wait_ge(w1_ready, 2)
                else:
                    pe.wait_ge(gelu_done, n - (1 if A is A_EARLY else 3))
                if isinstance(c, int) and c == 3 and e == 0:
                    pe.wait_ge(y_ready, 2)
                    pe.wait_ge(xT_ready, NCH)
                xs = xT_all[:, bass.ts(c, CH)]
                mm(A[e % 4][:, :], w1_hi[:, e, :], xs, start=True, stop=False)
                mm(A[e % 4][:, :], w1_lo[:, e, :], xs, start=False, stop=True).then_inc(mm1_done, 1)

            def project_pair(c, k):
                p = PAIRS * c + k
                if is_first(c) and k < 2:
                    if k == 0:
                        pe.wait_ge(w2_ld, 16)
                        pe.wait_ge(sT_ready, 3)
                        pe.wait_ge(xT_ready, 4)
                    else:
                        pe.wait_ge(g_ready, B)
                else:
                    pe.wait_ge(weighted, p - 1)
                pe.wait_ge(gelu_done, 2 * p + 2)
                for i in range(2):
                    e = 2 * k + i
                    ins = mm(Y_PS[k % 2][64 * i:64 * i + 64, :], w2_sb[:, e, :], act_sb[:, e % 4, :], start=True, stop=True)
                ins.then_inc(mm2_done, 1)

            def transpose_out(c, OT_PS):
                pe.wait_ge(added, 3 * c + 3)
                if is_first(c):
                    pe.wait_ge(h2_ready, B)
                else:
                    pe.wait_ge(y_ready, c)
                if OT_PS is OT_LATE and isinstance(c, int):
                    pe.wait_ge(z_ready, 3)
                for jj in range(4):
                    ins = nc.tensor.transpose(OT_PS[:, P * jj:P * jj + P], fin_sb[:, P * jj:P * jj + P], ident_sb[:, :])
                ins.then_inc(ot_done, 1)

            def moe(c, k, A):
                hidden(c, 2 * k, A)
                hidden(c, 2 * k + 1, A)
                if k:
                    project_pair(c, k - 1)
                else:
                    project_pair(c - 1, PAIRS - 1)

            keep_warm(1)
            pe.wait_ge(weff_ready, 4)
            tokenize(0)
            tokenize(1, range(0, 1))
            pe.wait_ge(wgc_ready, 1)
            pe.wait_ge(id_ld, 16)
            transpose_h(0)
            project_g(0)
            tokenize(1, range(1, 7))
            transpose_s(0)
            tokenize(1, range(7, 8))
            pe.wait_ge(wo_ready, 1)
            project_o(0)
            transpose_h(1)
            project_g(1)
            tokenize(2)
            transpose_x(0, 0)
            transpose_s(1)
            transpose_x(0, 1)
            transpose_h(2)
            project_o(1)
            project_g(2)
            pe.wait_ge(gw_ready, 1)
            gate_logits(0)
            tokenize(3)
            transpose_x(1, 0)
            transpose_x(1, 1)
            transpose_s(2)
            transpose_h(3)
            gate_logits(1)
            project_o(2)
            project_g(3)
            hidden(0, 0, A_EARLY)
            hidden(0, 1, A_EARLY)
            transpose_cw(0)
            moe(0, 1, A_EARLY)
            transpose_cw(1)
            moe(0, 2, A_EARLY)
            moe(0, 3, A_EARLY)
            transpose_s(3)
            moe(1, 0, A_EARLY)
            project_o(3)
            moe(1, 1, A_EARLY)
            transpose_x(2, 0)
            moe(1, 2, A_EARLY)
            transpose_x(2, 1)
            moe(1, 3, A_EARLY)
            transpose_out(0, OT_EARLY)
            gate_logits(2)
            transpose_cw(2)
            moe(2, 0, A_EARLY)
            moe(2, 1, A_EARLY)
            transpose_cw(3)
            transpose_x(3, 0)
            moe(2, 2, A_EARLY)
            transpose_out(1, OT_EARLY)
            transpose_x(3, 1)
            moe(2, 3, A_EARLY)
            gate_logits(3)
            moe(3, 0, A_LATE)
            moe(3, 1, A_LATE)
            transpose_out(2, OT_LATE)
            moe(3, 2, A_LATE)
            transpose_cw(4)
            moe(3, 3, A_LATE)
            transpose_cw(5)
            moe(4, 0, A_LATE)
            moe(4, 1, A_LATE)
            transpose_cw(6)
            moe(4, 2, A_LATE)
            transpose_out(3, OT_LATE)
            moe(4, 3, A_LATE)
            transpose_cw(7)
            with pe.Fori(5, NCH) as c:
                moe(c, 0, A_LATE)
                moe(c, 1, A_LATE)
                moe(c, 2, A_LATE)
                transpose_out(c - 1, OT_LATE)
                moe(c, 3, A_LATE)
            pe.wait_ge(weighted, PAIRS * NCH - 2)
            pe.wait_ge(gelu_done, E * NCH)
            for half in range(2):
                cols = slice(256 * half, 256 * half + 256)
                for i in range(2):
                    e = E - 2 + i
                    ins = mm(LAST_Y_PS[half][64 * i:64 * i + 64, cols], w2_sb[:, e, :], act_sb[:, e % 4, cols],
                             start=True, stop=True)
                ins.then_inc(last_mm2, 1)
            pe.wait_ge(fold_ready, 1)
            pe.wait_ge(y_ready, NCH - 1)

            def fold(half, src, first):
                for j in range(2):
                    ins = mm(FOLD_PS[half][:, D * j:D * j + D], src[:, 256 * half + P * j:256 * half + P * j + P],
                             fold_sb[:, :], start=first and j == 0, stop=not first and j == 1, skip_group_check=True)
                return ins

            for half in range(2):
                pe.wait_ge(last_weighted, half + 1)
                fold(half, yw_sb[:, PAIRS - 1, :], True)
            pe.wait_ge(last_added, 1)
            for half in range(2):
                fold(half, fin_sb, False).then_inc(folded, 1)


_INS = {"x": "x", "W": "L0_tok_W", "wg": "L0_attn_wg", "wo": "L0_attn_wo", "gn_bias": "L0_attn_gn_bias",
        "attn_bias": "L0_attn_bias", "gate_w": "L0_ffn_gate_w", "gate_b": "L0_ffn_gate_b", "W1": "L0_ffn_W1",
        "b1": "L0_ffn_b1", "W2": "L0_ffn_W2", "b2": "L0_ffn_b2"}


def _constants(np):
    f, p = np.arange(NF)[:, None], np.arange(WIN)[None, :]
    angle = 2.0 * np.pi * ((f * p) % WIN) / WIN
    table = np.concatenate([np.cos(angle), -np.sin(angle)]) / np.sqrt(WIN)
    half = np.eye(2)
    return {
        "dft": np.ascontiguousarray(np.kron(np.eye(DLO), table).reshape(DLO * G, DLO, 2, 2, 4).transpose(0, 3, 1, 2, 4)
                                    ).reshape(DLO * G, DLO * WIN).astype(np.float32),
        "ident": np.eye(P, dtype=np.float32),
        "center": np.kron(half, np.eye(D) - 1.0 / D).astype(np.float32),
        "rank": (E - np.arange(E, dtype=np.float32))[None, :],
    }


def kernel(**inputs):
    import numpy as np
    import concourse.bacc as bacc
    from concourse.bass_utils import run_bass_kernel_spmd

    nc = bacc.Bacc("TRN2", target_bir_lowering=False, num_devices=1)
    data = {k: np.ascontiguousarray(inputs[v]) for k, v in _INS.items()}
    data.update(_constants(np))
    arrays, args = {}, {}
    for name, a in data.items():
        arrays[f"in_{name}"] = a
        args[name] = nc.dram_tensor(f"in_{name}", a.shape, mybir.dt.from_np(a.dtype), kind="ExternalInput").ap()
    out = nc.dram_tensor("out", (B, V * NWIN, D), F32, kind="ExternalOutput").ap()
    vit_layer(nc, out=out, **args)
    r = run_bass_kernel_spmd(nc, [arrays], core_ids=[0])
    return r.results[0]["out"]
```
